# Optimizing a Trainium2 kernel written in Bass

```python
import numpy as np
import jax
import jax.numpy as jnp

def _softmax(x, axis=-1):
    return jax.nn.softmax(x, axis=axis)

def _gelu(x):
    return jax.nn.gelu(x, approximate=True)

def _silu(x):
    return jax.nn.silu(x)

def _sigmoid(x):
    return jax.nn.sigmoid(x)

def _layernorm(x, axis=-1, eps=1e-05):
    m = jnp.mean(x, axis=axis, keepdims=True)
    v = jnp.var(x, axis=axis, keepdims=True)
    return (x - m) / jnp.sqrt(v + eps)

def _scatter_add(tgt, idx, src, axis=0):
    return tgt.at[idx].add(src)

def _segment_sum(src, seg, n):
    return jax.ops.segment_sum(src, seg, n)
kernel_name = 'mk_sandwich_d1_jaxref_r8_1a6905'

def setup_inputs(seed: int=0):
    np.random.seed(seed)
    _w = jnp.asarray

    def _L0_attn_setup():
        import jax, jax.numpy as jnp
        import numpy as np
        B, N, D = (2, 256, 128)
        H, DH = (16, 64)
        key = jax.random.key(seed)
        ks = jax.random.split(key, 5)
        s = 0.02
        return {'x': jax.random.normal(ks[0], (B, N, D), dtype=jnp.float32), 'W_w': jax.random.normal(ks[1], (3 * H * DH, D), dtype=jnp.float32) * s, 'W_b': jax.random.normal(ks[2], (3 * H * DH,), dtype=jnp.float32) * s, 'out_w': jax.random.normal(ks[3], (D, H * DH), dtype=jnp.float32) * s, 'out_b': jax.random.normal(ks[4], (D,), dtype=jnp.float32) * s}
    _L0_attn_in = _L0_attn_setup()

    def _L0_ffn_setup():
        import jax, jax.numpy as jnp
        import numpy as np
        from jax import lax
        T, B, I, M, O = (32, 64, 128, 128, 128)

        def _xavier(key, shape):
            fan_out, fan_in = shape
            limit = float(np.sqrt(6.0 / (fan_in + fan_out)))
            return jax.random.uniform(key, shape, jnp.float32, -limit, limit)
        key = jax.random.key(seed)
        ks = jax.random.split(key, 9)
        x = jax.random.normal(ks[0], (T, B, I), jnp.float32)
        return {'x': x, 'wf': _xavier(ks[1], (M, I)), 'uf': _xavier(ks[2], (M, M)), 'bf': jnp.zeros((M,), jnp.float32), 'wi': _xavier(ks[3], (M, I)), 'ui': _xavier(ks[4], (M, M)), 'bi': jnp.zeros((M,), jnp.float32), 'wc': _xavier(ks[5], (M, I)), 'uc': _xavier(ks[6], (M, M)), 'bc': jnp.zeros((M,), jnp.float32), 'wo': _xavier(ks[7], (O, I)), 'uo': _xavier(ks[8], (O, M)), 'bo': jnp.zeros((O,), jnp.float32), 'in_c': jnp.zeros((M,), jnp.float32)}
    _L0_ffn_in = _L0_ffn_setup()
    _d = {'L0_attn_x': _L0_attn_in['x'], 'L0_attn_W_w': _L0_attn_in['W_w'], 'L0_attn_W_b': _L0_attn_in['W_b'], 'L0_attn_out_w': _L0_attn_in['out_w'], 'L0_attn_out_b': _L0_attn_in['out_b'], 'L0_ffn_wf': _L0_ffn_in['wf'], 'L0_ffn_uf': _L0_ffn_in['uf'], 'L0_ffn_bf': _L0_ffn_in['bf'], 'L0_ffn_wi': _L0_ffn_in['wi'], 'L0_ffn_ui': _L0_ffn_in['ui'], 'L0_ffn_bi': _L0_ffn_in['bi'], 'L0_ffn_wc': _L0_ffn_in['wc'], 'L0_ffn_uc': _L0_ffn_in['uc'], 'L0_ffn_bc': _L0_ffn_in['bc'], 'L0_ffn_wo': _L0_ffn_in['wo'], 'L0_ffn_uo': _L0_ffn_in['uo'], 'L0_ffn_bo': _L0_ffn_in['bo'], 'L0_ffn_in_c': _L0_ffn_in['in_c']}
    _x0 = _d['L0_attn_x']
    _d['L0_attn_x'] = jax.random.normal(jax.random.fold_in(jax.random.key(seed), 1), (1, 2048, 128), dtype=_x0.dtype)
    del _x0
    return _d

def reference(L0_attn_x, L0_attn_W_w, L0_attn_W_b, L0_attn_out_w, L0_attn_out_b, L0_ffn_wf, L0_ffn_uf, L0_ffn_bf, L0_ffn_wi, L0_ffn_ui, L0_ffn_bi, L0_ffn_wc, L0_ffn_uc, L0_ffn_bc, L0_ffn_wo, L0_ffn_uo, L0_ffn_bo, L0_ffn_in_c):

    def _L0_attn_ref(x, W_w, W_b, out_w, out_b):
        import jax, jax.numpy as jnp
        import numpy as np
        B, N, D = (2, 256, 128)
        H, DH = (16, 64)
        b, n, _ = x.shape
        qkv = x @ W_w.T + W_b
        Q, K, V = jnp.split(qkv, 3, axis=-1)
        split_heads = lambda t: t.reshape(b, n, H, DH).transpose(0, 2, 1, 3)
        q, k, v = map(split_heads, (Q, K, V))
        scale = DH ** (-0.5)
        dots = jnp.einsum('bhik,bhjk->bhij', q, k) * scale
        attn = jax.nn.softmax(dots, axis=-1)
        out = jnp.einsum('bhij,bhjk->bhik', attn, v)
        out = out.transpose(0, 2, 1, 3).reshape(b, n, H * DH)
        return out @ out_w.T + out_b

    def _L0_ffn_ref(x, wf, uf, bf, wi, ui, bi, wc, uc, bc, wo, uo, bo, in_c):
        import jax, jax.numpy as jnp
        import numpy as np
        from jax import lax
        T, B, I, M, O = (32, 64, 128, 128, 128)

        def _xavier(key, shape):
            fan_out, fan_in = shape
            limit = float(np.sqrt(6.0 / (fan_in + fan_out)))
            return jax.random.uniform(key, shape, jnp.float32, -limit, limit)
        batch = x.shape[1]
        c0 = jnp.broadcast_to(in_c, (batch, in_c.shape[0]))

        def step(c, xt):
            ft = jax.nn.sigmoid(xt @ wf.T + c @ uf.T + bf)
            it = jax.nn.sigmoid(xt @ wi.T + c @ ui.T + bi)
            gt = jnp.tanh(xt @ wc.T + c @ uc.T + bc)
            c = ft * c + it * gt
            return (c, None)
        c_final, _ = lax.scan(step, c0, x)
        h = jnp.tanh(jnp.einsum('tbi,oi->tbo', x, wo) + c_final @ uo.T + bo)
        return h
    x = L0_attn_x
    x = x + _layernorm(_L0_attn_ref(_layernorm(x, axis=-1), L0_attn_W_w, L0_attn_W_b, L0_attn_out_w, L0_attn_out_b), axis=-1)
    x = x + _layernorm(_L0_ffn_ref(_layernorm(x, axis=-1), L0_ffn_wf, L0_ffn_uf, L0_ffn_bf, L0_ffn_wi, L0_ffn_ui, L0_ffn_bi, L0_ffn_wc, L0_ffn_uc, L0_ffn_bc, L0_ffn_wo, L0_ffn_uo, L0_ffn_bo, L0_ffn_in_c), axis=-1)
    return x

_drawn_inputs = setup_inputs


def setup_inputs(seed=0):
    import zlib

    import numpy as np

    out = dict(_drawn_inputs(seed))
    spreads = {'L0_ffn_bf': (0.0, 2.0),
     'L0_ffn_bi': (0.0, 0.8),
     'L0_ffn_bc': (0.0, 0.451),
     'L0_ffn_bo': (0.0, 0.1),
     'L0_ffn_in_c': (0.0, 0.1)}
    factors = {'L0_ffn_wf': 14.426, 'L0_ffn_uf': 64.0, 'L0_ffn_ui': 8.0, 'L0_ffn_uc': 2.999}
    for name, (base, spread) in spreads.items():
        noise = np.random.default_rng([zlib.crc32(name.encode()), seed]).standard_normal(out[name].shape)
        drawn = base * np.exp(spread * noise) if base else spread * noise
        out[name] = jnp.asarray(drawn.astype(out[name].dtype))
    for name, factor in factors.items():
        out[name] = (out[name] * factor).astype(out[name].dtype)
    return out
```

```python
from contextlib import ExitStack

import concourse.bass as bass
from concourse import mybir

F32 = mybir.dt.float32
F32R = mybir.dt.float32r
ACT = mybir.ActivationFunctionType
ALU = mybir.AluOpType
AX = mybir.AxisListType

P = 128
DH = 64
CH = 512
EPS = 1e-5



class Plan:

    def __init__(self, tokens, heads):
        self.tokens = tokens
        self.tiles = tokens // P
        self.qblk = 1024
        self.blocks = tokens // self.qblk
        self.chunks = tokens // CH
        self.pairs = heads // 2
        self.head_steps = self.blocks * self.tiles
        self.steps = 2 * self.head_steps
        assert self.blocks == 2 and self.tiles == 16 and self.chunks == 4

    def units(self, last):
        by = [[] for _ in range(self.steps)]
        half = self.tiles // 2 * self.chunks

        def spread(units, first, count):
            for i, u in enumerate(units):
                by[first + i * count // len(units)].append(u)

        for e in range(2):
            s = e * self.head_steps
            spread([("max", e, 1, i) for i in range(half)], s, 12)
            by[s + 12].append(("max_row", e, 1))
            if e == 0:
                by[s + 12].append(("out", 0))
                by[s + 12].append(("out", 1))
                by[s + 13].append(("out", 2))
                by[s + 14].append(("out", 3))
            elif not last:
                for g in range(4):
                    by[s + 13 + g].append(("value", g))
            if e == 0 or not last:
                spread([("max", 1 - e, 0, i) for i in range(half)], s + 13, 15)
                by[s + 28].append(("max_row", 1 - e, 0))
            if e == 0 and not last:
                for i in range(8):
                    by[s + 22 + i].append(("project", i // 4, i % 4))
        return by


def first_in(units, kind, *args):
    flat = [u for step in units for u in step]
    return next(i for i, u in enumerate(flat) if u[:1 + len(args)] == (kind,) + args)


def last_in(units, kind, *args):
    flat = [u for step in units for u in step]
    return max(i for i, u in enumerate(flat) if u[:1 + len(args)] == (kind,) + args)


def bass_attention_then_gated_step(nc, x, w_pair, w_out, w_ffn, vecs, ident_in, y):
    plan = Plan(x.shape[0], 2 * w_pair.shape[0])
    N, T, QB, PAIRS = plan.tokens, plan.tiles, plan.qblk, plan.pairs
    S, HS = plan.steps, plan.head_steps
    SCALE = float(DH) ** -0.5
    units, units_last = plan.units(False), plan.units(True)
    U = sum(len(s) for s in units)
    HALF = T // 2 * plan.chunks
    U0 = 4 + 8 + 4 + HALF + 1
    WQ, WK, WV, BV, BQ, BK = 0, P, 2 * P, 3 * P, 4 * P, 4 * P + 1
    assert U % 2 == 0 and (U0 + U) % 2 == U0 % 2
    NSTAT = 6

    with ExitStack() as ctx:
        def sb(name, shape, dt=F32):
            return ctx.enter_context(nc.sbuf_tensor(name, shape, dt))

        def sem(name):
            return ctx.enter_context(nc.semaphore(name))

        staged = sb("staged", [P, 4, N], F32R)
        keys_full = [sb(f"keys_full{e}", [P, N], F32R) for e in range(2)]
        keys_hi = [sb(f"keys_hi{e}", [P, N], F32R) for e in range(2)]
        queries_hi = [sb(f"queries_hi{e}", [P, N], F32R) for e in range(2)]
        queries_lo = [sb(f"queries_lo{e}", [P, N], F32R) for e in range(2)]
        own = [slice(0, DH), slice(DH, P)]
        other = [slice(DH, P), slice(0, DH)]
        max_row_at = [DH, 0]
        values_hi = [sb(f"values_hi{e}", [P, T, 2 * DH], F32R) for e in range(2)]
        values_lo = [sb(f"values_lo{e}", [P, T, DH + 1], F32R) for e in range(2)]
        values_full = sb("values_full", [P, T, P])
        probs = sb("probs", [P, 2, QB])
        probs_hi = sb("probs_hi", [P, 4, QB], F32R)
        probs_lo = sb("probs_lo", [P, 4, QB], F32R)
        numer = sb("numer", [P, QB])
        recip = sb("recip", [P, QB])
        sums = sb("sums", [P, QB // P])
        recips = sb("recips", [P, QB // P])
        heads_out = sb("heads_out", [P, N])
        attn = sb("attn", [P, N])
        xnT = sb("xnT", [P, N])
        wp = sb("wp", [P, w_pair.shape[2]])
        wo = sb("wo", [P, P])
        vec = sb("vec", [P, 6])
        ident = sb("ident", [P, P])
        chunk_max = sb("chunk_max", [P, 2, HALF])
        row_max = sb("row_max", [P, 2, T // 2])
        minus_max = sb("minus_max", [T // 2, P], F32R)
        stats = sb("stats", [P, T, NSTAT])
        moments = sb("moments", [P, T, 2])
        std = sb("std", [P, T])
        rstd = sb("rstd", [P, T])
        gate_bias = sb("gate_bias", [P, 3])
        eps = sb("eps", [P, 1])

        x_sb = staged[:, 0, :].bitcast(F32).rearrange("p (t d) -> p t d", d=P)
        xn = staged[:, 1, :].bitcast(F32).rearrange("p (t d) -> p t d", d=P)
        y_sb = xn
        hT = staged[:, 2, :].bitcast(F32)
        ffn = staged[:, 3, 0:8 * P].bitcast(F32)
        mix = recip
        forget = probs[:, :, :].rearrange("p a c -> p (a c)")
        take = values_full[:, :, :].rearrange("p a c -> p (a c)")
        fresh = heads_out
        new_c = attn
        CONST, OUT, TURN, ZT, GATE, HID, YT = 0, 1, 5, 9, 13, 25, 29

        ps = ctx.enter_context(nc.psum_tensor("ps", [P, 8, CH], F32))
        AUX, PV = 6, 4

        def aux(k):
            return ps[:, AUX + k % 2, :]

        def bank(v):
            return ps[:, v % 8, :]

        eps_set = sem("eps_set")
        x_in, const_in, wp_in, wo_in = sem("x_in"), sem("const_in"), sem("wp_in"), sem("wo_in")
        head_in = [sem("head0_in"), sem("head1_in")]
        max_in = [sem("max0_in"), sem("max1_in")]
        zeroed, consts_set = sem("zeroed"), sem("consts_set")
        xn_ready = sem("xn_ready")
        aux_full, aux_free = sem("aux_full"), sem("aux_free")
        scores_ready = sem("scores_ready")
        probs_ready, hi_ready, lo_ready = sem("probs_ready"), sem("hi_ready"), sem("lo_ready")
        pv_done = sem("pv_done")
        numer_ready = sem("numer_ready")
        sums_in, recips_ready = sem("sums_in"), sem("recips_ready")
        recip_row_in, recip_in = sem("recip_row_in"), sem("recip_in")
        heads_ready = sem("heads_ready")
        stage_hi = sem("stage_hi")
        v_hi, v_lo = sem("v_hi"), sem("v_lo")
        row_max_ready = sem("row_max_ready")
        ln_stat, ln_mom, ln_std, ln_rstd = sem("ln_stat"), sem("ln_mom"), sem("ln_std"), sem("ln_rstd")
        gate_const, gate_const_ready = sem("gate_const"), sem("gate_const_ready")
        out_full, attn_ready, turned = sem("out_full"), sem("attn_ready"), sem("turned")
        x1_ready = sem("x1_ready")
        z_turned, zT_ready = sem("z_turned"), sem("zT_ready")
        gate_full, gates_ready, mixed, c_ready = sem("gate_full"), sem("gates_ready"), sem("mixed"), sem("c_ready")
        h_full, h_ready, h_turned = sem("h_full"), sem("h_ready"), sem("h_turned")
        norms = sem("norms")
        y_ready, y_out = sem("y_ready"), sem("y_out")
        PV0 = 4
        MEMSETS = 10

        def st(n):
            b = 2 * (n % 2)
            return ps[:, b:b + 2, :]

        block = ctx.enter_context(nc.Block())

        @block.sync
        def _(sp):
            def assemble(e):
                for dst, rows, part in ((keys_full, own, 0), (keys_full, other, 1), (keys_hi, own, 0),
                                        (queries_hi, own, 2), (queries_hi, other, 2), (queries_lo, own, 3)):
                    sp.dma_start(dst[e][rows[e], :].bitcast(F32),
                                 staged[own[e], part, :].bitcast(F32)).then_inc(head_in[e], 16)

            def row_in(e, b, u):
                sp.wait_ge(aux_free, u + 1)
                r = max_row_at[e]
                sp.dma_start(queries_lo[e][r:r + 1, b * QB:(b + 1) * QB].bitcast(F32)
                             .rearrange("a (t q) -> a t q", q=P),
                             minus_max[:, :].bitcast(F32)).then_inc(max_in[e], 16)

            def spread_recips(block):
                sp.wait_ge(numer_ready, block + 2)
                sp.dma_start(sums[:, :], numer[DH:DH + 1, :].rearrange("a (p c) -> a p c", p=P)).then_inc(sums_in, 16)
                sp.wait_ge(recips_ready, block + 2)
                sp.dma_start(recip[DH:DH + 1, :].rearrange("a (p c) -> a p c", p=P), recips[:, :]).then_inc(recip_row_in, 16)
                sp.wait_ge(recip_row_in, block * 16 + 32)
                sp.dma_start(recip[0:DH, :], recip[DH:DH + 1, :].unsqueeze(1).to_broadcast([1, DH, QB])).then_inc(recip_in, 16)

            sp.dma_start(x_sb, x.rearrange("(t p) d -> p t d", p=P)).then_inc(x_in, 16)
            sp.dma_start(ident[:, :], ident_in).then_inc(const_in, 16)
            sp.dma_start(wp[:, :], w_pair[0]).then_inc(wp_in, 16)
            sp.dma_start(wo[:, :], w_out[0:P, :]).then_inc(wo_in, 16)
            sp.dma_start(vec[:, :], vecs).then_inc(const_in, 16)
            sp.wait_ge(aux_free, 4 + 8)
            sp.wait_ge(consts_set, MEMSETS)
            assemble(0)
            row_in(0, 0, U0 - 1)

            def pair(p, units, last):
                base = p * U + U0
                if not last:
                    sp.wait_ge(aux_full, base)
                    sp.dma_start(wp[:, :], w_pair[bass.ds(p + 1, 1)].rearrange("a p n -> (a p) n")
                                 ).then_inc(wp_in, 16)
                sp.wait_ge(scores_ready, p * S + 1)
                assemble(1)
                spread_recips(p * 4 - 1)
                row_in(0, 1, base + first_in(units, "max_row", 0, 1))
                sp.wait_ge(aux_full, base + last_in(units, "out") + 1)
                sp.dma_start(wo[:, :], w_out[bass.ds(p * P, P), :]).then_inc(wo_in, 16)
                spread_recips(p * 4)
                row_in(1, 0, base + first_in(units, "max_row", 1, 0))
                if not last:
                    sp.wait_ge(aux_full, base + first_in(units, "max", 1, 1) + 2)
                    assemble(0)
                spread_recips(p * 4 + 1)
                row_in(1, 1, base + first_in(units, "max_row", 1, 1))
                spread_recips(p * 4 + 2)
                if not last:
                    row_in(0, 0, base + first_in(units, "max_row", 0, 0))

            with sp.Fori(0, PAIRS - 1) as p:
                pair(p, units, False)
            pair(PAIRS - 1, units_last, True)

            spread_recips(PAIRS * 4 - 1)
            sp.wait_ge(head_in[0], 96 * PAIRS)
            sp.wait_ge(head_in[1], 96 * PAIRS)
            sp.dma_start(ffn, w_ffn).then_inc(const_in, 16)
            sp.dma_start(x_sb, x.rearrange("(t p) d -> p t d", p=P)).then_inc(x_in, 16)
            for c in range(4):
                sp.wait_ge(y_ready, c + 1)
                sp.dma_start(y.rearrange("(t p) d -> p t d", p=P)[:, 4 * c:4 * c + 4, :],
                             xn[:, 4 * c:4 * c + 4, :]).then_inc(y_out, 16)
            sp.wait_ge(y_out, 64)

        @block.gpsimd
        def _(pool):
            for e in range(2):
                nc.gpsimd.memset(keys_hi[e][:, :].bitcast(F32), 0.0).then_inc(zeroed, 1)
                nc.gpsimd.memset(queries_lo[e][:, :].bitcast(F32), 0.0).then_inc(consts_set, 1)
                nc.gpsimd.memset(values_hi[e][:, :, DH:2 * DH].bitcast(F32), 1.0).then_inc(consts_set, 1)
                nc.gpsimd.memset(values_lo[e][:, :, DH:DH + 1].bitcast(F32), 0.0).then_inc(consts_set, 1)
            nc.gpsimd.memset(attn[:, :], 0.0).then_inc(consts_set, 1)
            nc.gpsimd.memset(probs[:, :, :], 0.0).then_inc(pv_done, PV0)
            nc.gpsimd.memset(numer[0:DH, :], 0.0).then_inc(consts_set, 1)
            nc.gpsimd.memset(heads_out[:, :], 0.0).then_inc(heads_ready, 1)

        @block.scalar
        def _(act):
            act.wait_ge(ln_mom, 1)
            act.wait_ge(eps_set, 1)
            nc.scalar.activation(std[:, :], moments[:, :, 1], ACT.Sqrt, bias=eps[:, 0:1]).then_inc(ln_std, 1)

            def exp_step(g, n):
                first = isinstance(g, int) and g < 2
                act.wait_ge(scores_ready, g + 1)
                if first:
                    act.wait_ge(pv_done, PV0)
                else:
                    act.wait_ge(lo_ready, g - 1)
                nc.scalar.activation(probs[:, n % 2, :].rearrange("p (b c) -> p b c", c=CH), st(n),
                                     ACT.Exp, scale=SCALE).then_inc(probs_ready, 1)
                act.wait_ge(probs_ready, g + 1)
                if not first:
                    act.wait_ge(pv_done, PV0 + g - 3)
                nc.scalar.copy(probs_hi[:, n % 4, :], probs[:, n % 2, :]).then_inc(hi_ready, 1)

            def value_hi(e):
                nc.scalar.copy(values_hi[e][:, :, 0:DH], values_full[:, :, e * DH:(e + 1) * DH]).then_inc(v_hi, 1)

            act.wait_ge(aux_free, 16)
            act.wait_ge(consts_set, MEMSETS)
            value_hi(0)
            exp_step(0, 0)
            exp_step(1, 1)

            def pair(p, units, last):
                for n in range(S):
                    g = p * S + n
                    if n == 2:
                        act.wait_ge(pv_done, PV0 + p * S)
                        value_hi(1)
                    if n == HS + 20 and not last:
                        act.wait_ge(aux_free, p * U + U0 + last_in(units, "value") + 1)
                        act.wait_ge(pv_done, PV0 + p * S + HS)
                        value_hi(0)
                    if not (last and n + 2 >= S):
                        exp_step(g + 2, n + 2)
                    if n % T == T - 1:
                        act.wait_ge(pv_done, PV0 + g + 1)
                        act.wait_ge(heads_ready, p * 4 + n // T + 2)
                        nc.scalar.copy(numer[0:DH + 1, :].rearrange("p (b c) -> p b c", c=CH),
                                       ps[0:DH + 1, PV:PV + 2, :]).then_inc(numer_ready, 1)

            with act.Fori(0, PAIRS - 1) as p:
                pair(p, units, False)
            pair(PAIRS - 1, units_last, True)

            def std_of(k):
                act.wait_ge(ln_mom, 2 + k)
                nc.scalar.activation(std[:, 4 * (k % 4):4 * (k % 4) + 4], moments[:, 4 * (k % 4):4 * (k % 4) + 4, 1],
                                     ACT.Sqrt, bias=eps[:, 0:1]).then_inc(ln_std, 1)

            for k in range(8):
                std_of(k)
            for c in range(4):
                act.wait_ge(z_turned, c + 1)
                nc.scalar.copy(xnT[:, c * CH:(c + 1) * CH], bank(ZT + c)).then_inc(zT_ready, 1)
            act.wait_ge(gate_const_ready, 1)
            for c in range(4):
                for k, (func, dst) in enumerate(((ACT.Sigmoid, forget), (ACT.Sigmoid, take), (ACT.Tanh, fresh))):
                    act.wait_ge(gate_full, 3 * c + k + 1)
                    nc.scalar.activation(dst[:, c * CH:(c + 1) * CH], bank(GATE + 3 * c + k), func,
                                         bias=gate_bias[:, k:k + 1]).then_inc(gates_ready, 1)
            for c in range(4):
                act.wait_ge(h_full, c + 1)
                nc.scalar.activation(hT[:, c * CH:(c + 1) * CH], bank(HID + c), ACT.Tanh,
                                     bias=vec[:, 3:4]).then_inc(h_ready, 1)
            for k in range(8, 12):
                std_of(k)

        @block.vector
        def _(ve):
            nc.vector.memset(eps[:, :], EPS).then_inc(eps_set, 1)
            nc.vector.memset(numer[DH:DH + 1, :], 1.0).then_inc(numer_ready, 1)
            ve.wait_ge(x_in, 16)
            for t in range(T):
                nc.vector.bn_stats(stats[:, t, :], x_sb[:, t, :]).then_inc(ln_stat, 1)
            ve.wait_ge(ln_stat, T)
            for t in range(T):
                ins = nc.vector.bn_aggr(moments[:, t, :], stats[:, t, :])
            ins.then_inc(ln_mom, 1)
            ve.wait_ge(ln_std, 1)
            nc.vector.reciprocal(rstd[:, :], std[:, :]).then_inc(ln_rstd, 1)
            ve.wait_ge(ln_rstd, 1)
            for t in range(T):
                ins = nc.vector.tensor_scalar(xn[:, t, :], x_sb[:, t, :], moments[:, t, 0:1], rstd[:, t:t + 1],
                                              ALU.subtract, ALU.mult)
                if t % 4 == 3:
                    ins.then_inc(xn_ready, 1)

            def project(u, k, part, c, count):
                cols = slice(c * CH, (c + 1) * CH)
                b = wp[:, BQ:BQ + 1] if part else wp[:, BK:BK + 1]
                ve.wait_ge(aux_full, u + 1)
                nc.vector.tensor_scalar(staged[:, 2 * part, cols], aux(k), b, None, ALU.add).then_inc(stage_hi, 1)
                ve.wait_ge(stage_hi, count)
                nc.vector.scalar_tensor_tensor(out=staged[:, 2 * part + 1, cols], in0=aux(k), scalar=b,
                                               in1=staged[:, 2 * part, cols].bitcast(F32),
                                               op0=ALU.add, op1=ALU.subtract).then_inc(aux_free, 1)

            def value(u, k, g):
                ve.wait_ge(aux_full, u + 1)
                nc.vector.tensor_tensor(values_full[:, 4 * g:4 * g + 4, :],
                                        aux(k).rearrange("p (t d) -> p t d", d=P),
                                        wp[:, BV:BV + P].unsqueeze(1).to_broadcast([P, 4, P]),
                                        ALU.add).then_inc(aux_free, 1)

            def chunk_of_max(u, k, b, i):
                ve.wait_ge(aux_full, u + 1)
                nc.vector.tensor_reduce(chunk_max[:, b, i:i + 1], aux(k), AX.X, ALU.max).then_inc(aux_free, 1)
                if i == HALF - 1:
                    ve.wait_ge(aux_free, u + 1)
                    nc.vector.tensor_reduce(row_max[:, b, :],
                                            chunk_max[:, b, :].rearrange("p (t c) -> p t c", c=plan.chunks),
                                            AX.X, ALU.max).then_inc(row_max_ready, 1)

            def write_row(u, k):
                ve.wait_ge(aux_full, u + 1)
                nc.vector.tensor_scalar(minus_max[:, :], aux(k)[0:T // 2, 0:P], -1.0, None,
                                        ALU.mult).then_inc(aux_free, 1)

            def value_lo(e, count):
                ve.wait_ge(v_hi, count)
                nc.vector.tensor_tensor(values_lo[e][:, :, 0:DH], values_full[:, :, e * DH:(e + 1) * DH],
                                        values_hi[e][:, :, 0:DH].bitcast(F32), ALU.subtract).then_inc(v_lo, 1)

            def lo_step(g, n):
                ve.wait_ge(hi_ready, g + 1)
                if not (isinstance(g, int) and g == 0):
                    ve.wait_ge(pv_done, PV0 + g - 3)
                nc.vector.tensor_tensor(probs_lo[:, n % 4, :], probs[:, n % 2, :],
                                        probs_hi[:, n % 4, :].bitcast(F32), ALU.subtract).then_inc(lo_ready, 1)

            for c in range(4):
                ve.wait_ge(aux_full, c + 1)
                nc.vector.tensor_copy(xnT[:, c * CH:(c + 1) * CH], aux(c)).then_inc(aux_free, 1)
            ve.wait_ge(zeroed, 2)
            for e in range(2):
                r = max_row_at[e]
                nc.vector.memset(keys_hi[e][r:r + 1, :].bitcast(F32), 1.0).then_inc(consts_set, 1)
            ve.wait_ge(wp_in, 16)
            for i in range(8):
                project(4 + i, 4 + i, i // 4, i % 4, i + 1)
            for g in range(4):
                value(12 + g, 12 + g, g)
            value_lo(0, 1)
            for i in range(HALF):
                chunk_of_max(16 + i, 16 + i, 0, i)
            write_row(U0 - 1, U0 - 1)
            lo_step(0, 0)

            def recips_of(block):
                ve.wait_ge(sums_in, block * 16 + 32)
                nc.vector.reciprocal(recips[:, :], sums[:, :]).then_inc(recips_ready, 1)

            def normalise(block, i):
                e, b = i // 2, i % 2
                ve.wait_ge(recip_in, block * 16 + 32)
                ve.wait_ge(heads_ready, block + 2)
                nc.vector.tensor_tensor(heads_out[own[e], b * QB:(b + 1) * QB], numer[0:DH, :],
                                        recip[0:DH, :], ALU.mult).then_inc(heads_ready, 1)

            def unit(kind, args, p, u, k, units):
                if kind == "max":
                    e, b, i = args
                    chunk_of_max(u, k, b, i)
                elif kind == "max_row":
                    if args == [0, 1]:
                        ve.wait_ge(max_in[0], p * 32 + 16)
                    elif args == [1, 0]:
                        ve.wait_ge(max_in[0], p * 32 + 32)
                    elif args == [1, 1]:
                        ve.wait_ge(max_in[1], p * 32 + 16)
                    else:
                        ve.wait_ge(max_in[1], p * 32 + 32)
                    write_row(u, k)
                elif kind == "project":
                    part, c = args
                    if part == 0 and c == 0:
                        ve.wait_ge(head_in[0], p * 96 + 96)
                        ve.wait_ge(head_in[1], p * 96 + 96)
                    project(u, k, part, c, p * 8 + 9 + 4 * part + c)
                elif kind == "value":
                    if args[0] == 0:
                        ve.wait_ge(v_hi, p * 2 + 2)
                        ve.wait_ge(v_lo, p * 2 + 2)
                    value(u, k, args[0])
                elif kind == "out":
                    cols = slice(args[0] * CH, (args[0] + 1) * CH)
                    ve.wait_ge(consts_set, MEMSETS)
                    ve.wait_ge(aux_full, u + 1)
                    nc.vector.tensor_tensor(attn[:, cols], aux(k), attn[:, cols], ALU.add).then_inc(aux_free, 1)

            def pair(p, units, last):
                base, local = p * U + U0, 0
                for n in range(S):
                    g = p * S + n
                    for i in range(max(2, len(units[n]))):
                        if i < len(units[n]):
                            kind, *args = units[n][i]
                            unit(kind, args, p, base + local, U0 + local, units)
                            local += 1
                        if i == 1 and not (last and n + 1 >= S):
                            lo_step(g + 1, n + 1)
                    if n == 2:
                        value_lo(1, p * 2 + 2)
                    if n == HS + 20 and not last:
                        value_lo(0, p * 2 + 3)
                    if n % T == 2:
                        recips_of(p * 4 + n // T - 1)
                    if n % T == 6:
                        blk = n // T
                        if blk == 1:
                            ve.wait_ge(aux_full, base + last_in(units, "out") + 1)
                        normalise(p * 4 + blk - 1, (blk + 3) % 4)

            with ve.Fori(0, PAIRS - 1) as p:
                pair(p, units, False)
            pair(PAIRS - 1, units_last, True)
            recips_of(PAIRS * 4 - 1)
            normalise(PAIRS * 4 - 1, 3)

            ve.wait_ge(gate_const, 1)
            nc.vector.tensor_tensor(gate_bias[:, :], bank(CONST)[:, 0:3], vec[:, 0:3], ALU.add).then_inc(gate_const_ready, 1)
            for c in range(4):
                cols = slice(c * CH, (c + 1) * CH)
                ve.wait_ge(out_full, c + 1)
                nc.vector.scalar_tensor_tensor(out=attn[:, cols], in0=bank(OUT + c), scalar=vec[:, 5:6],
                                               in1=attn[:, cols], op0=ALU.add, op1=ALU.add).then_inc(attn_ready, 1)

            def tiles4(v):
                return bank(v).rearrange("p (t d) -> p t d", d=P)

            def moments_of(k, src):
                t0 = 4 * (k % 4)
                if k >= 4:
                    ve.wait_ge(norms, 4 * (k - 3))
                for j in range(4):
                    nc.vector.bn_stats(stats[:, t0 + j, :], src(j)).then_inc(ln_stat, 1)
                ve.wait_ge(ln_stat, T + 4 * (k + 1))
                for j in range(4):
                    ins = nc.vector.bn_aggr(moments[:, t0 + j, :], stats[:, t0 + j, :])
                ins.then_inc(ln_mom, 1)

            def rstd_of(k):
                t0 = 4 * (k % 4)
                ve.wait_ge(ln_std, 2 + k)
                nc.vector.reciprocal(rstd[:, t0:t0 + 4], std[:, t0:t0 + 4]).then_inc(ln_rstd, 1)
                ve.wait_ge(ln_rstd, 2 + k)

            def norm_tile(dst, src, t):
                return nc.vector.tensor_scalar(dst, src, moments[:, t, 0:1], rstd[:, t:t + 1],
                                               ALU.subtract, ALU.mult)

            ve.wait_ge(x_in, 32)
            for c in range(4):
                ve.wait_ge(turned, c + 1)
                moments_of(c, lambda j: tiles4(TURN + c)[:, j, :])
            for c in range(4):
                rstd_of(c)
                for j in range(4):
                    t = 4 * c + j
                    norm_tile(xn[:, t, :], tiles4(TURN + c)[:, j, :], t).then_inc(norms, 1)
                ve.wait_ge(norms, 4 * c + 4)
                nc.vector.tensor_tensor(x_sb[:, 4 * c:4 * c + 4, :], x_sb[:, 4 * c:4 * c + 4, :],
                                        xn[:, 4 * c:4 * c + 4, :], ALU.add).then_inc(x1_ready, 1)
            for c in range(4):
                ve.wait_ge(x1_ready, c + 1)
                moments_of(4 + c, lambda j: x_sb[:, 4 * c + j, :])
            for c in range(4):
                rstd_of(4 + c)
                for j in range(4):
                    t = 4 * c + j
                    norm_tile(xn[:, t, :], x_sb[:, t, :], t).then_inc(norms, 1)
            for c in range(4):
                cols, half = slice(c * CH, (c + 1) * CH), slice(c % 2 * CH, (c % 2 + 1) * CH)
                ve.wait_ge(gates_ready, 3 * (c + 1))
                if c >= 2:
                    ve.wait_ge(c_ready, c - 1)
                nc.vector.tensor_tensor(mix[:, half], take[:, cols], fresh[:, cols], ALU.mult).then_inc(mixed, 1)
                ve.wait_ge(mixed, c + 1)
                nc.vector.scalar_tensor_tensor(out=new_c[:, cols], in0=forget[:, cols], scalar=vec[:, 4:5],
                                               in1=mix[:, half], op0=ALU.mult, op1=ALU.add).then_inc(c_ready, 1)
            for c in range(4):
                ve.wait_ge(h_turned, c + 1)
                moments_of(8 + c, lambda j: tiles4(YT + c)[:, j, :])
            for c in range(4):
                rstd_of(8 + c)
                for j in range(4):
                    t = 4 * c + j
                    norm_tile(y_sb[:, t, :], tiles4(YT + c)[:, j, :], t).then_inc(norms, 1)
                ve.wait_ge(norms, 32 + 4 * c + 4)
                nc.vector.tensor_tensor(y_sb[:, 4 * c:4 * c + 4, :], y_sb[:, 4 * c:4 * c + 4, :],
                                        x_sb[:, 4 * c:4 * c + 4, :], ALU.add).then_inc(y_ready, 1)

        @block.tensor
        def _(pe):
            def turn4(dst, src):
                for j in range(4):
                    ins = nc.tensor.transpose(dst[:, j * P:(j + 1) * P], src(j), ident[:, :])
                return ins

            def project(u, k, part, c):
                pe.wait_ge(aux_free, u - 1)
                w = WQ if part else WK
                nc.tensor.matmul(aux(k), wp[:, w:w + P], xnT[:, c * CH:(c + 1) * CH],
                                 start=True, stop=True).then_inc(aux_full, 1)

            def value(u, k, g):
                pe.wait_ge(aux_free, u - 1)
                for j in range(4):
                    t = 4 * g + j
                    ins = nc.tensor.matmul(aux(k)[:, j * P:(j + 1) * P], xnT[:, t * P:(t + 1) * P], wp[:, WV:WV + P],
                                           start=True, stop=True)
                ins.then_inc(aux_full, 1)

            def chunk_scores(u, k, e, b, i):
                t, c = b * (T // 2) + i // plan.chunks, i % plan.chunks
                pe.wait_ge(aux_free, u - 1)
                nc.tensor.matmul(aux(k), queries_hi[e][:, t * P:(t + 1) * P], keys_full[e][:, c * CH:(c + 1) * CH],
                                 start=True, stop=True).then_inc(aux_full, 1)

            def turn_max(u, k, b, count):
                pe.wait_ge(aux_free, u - 1)
                pe.wait_ge(row_max_ready, count)
                nc.tensor.transpose(aux(k)[0:T // 2, 0:P], row_max[:, b, :], ident[:, :]).then_inc(aux_full, 1)

            def scores_chunk(g, n, c):
                hs = n % S
                e, b, jt = hs // HS, hs % HS // T, hs % T
                keys = slice(jt * P, (jt + 1) * P)
                cols = slice(b * QB + c * CH, b * QB + (c + 1) * CH)
                out = ps[:, 2 * (n % 2) + c, :]
                nc.tensor.matmul(out, keys_full[e][:, keys], queries_hi[e][:, cols], start=True, stop=False)
                return nc.tensor.matmul(out, keys_hi[e][:, keys], queries_lo[e][:, cols], start=False, stop=True)

            def pv_chunk(n, c):
                e, jt = n // HS, n % T
                first, final = jt == 0, jt == T - 1
                out = ps[:, PV + c, :]
                hi = probs_hi[:, n % 4, c * CH:(c + 1) * CH]
                nc.tensor.matmul(out, values_hi[e][:, jt, :], hi, start=first, stop=False)
                nc.tensor.matmul(out[0:DH + 1, :], values_lo[e][:, jt, :], hi, start=False, stop=False)
                return nc.tensor.matmul(out, values_hi[e][:, jt, :], probs_lo[:, n % 4, c * CH:(c + 1) * CH],
                                        start=False, stop=final)

            pe.wait_ge(const_in, 32)
            for c in range(4):
                pe.wait_ge(xn_ready, c + 1)
                if c >= 2:
                    pe.wait_ge(aux_free, c - 1)
                turn4(aux(c), lambda j: xn[:, 4 * c + j, :]).then_inc(aux_full, 1)
            pe.wait_ge(wp_in, 16)
            pe.wait_ge(aux_free, 4)
            for i in range(8):
                project(4 + i, 4 + i, i // 4, i % 4)
            for g in range(4):
                value(12 + g, 12 + g, g)
            pe.wait_ge(head_in[0], 96)
            for i in range(HALF):
                chunk_scores(16 + i, 16 + i, 0, 0, i)
            turn_max(U0 - 1, U0 - 1, 0, 1)
            pe.wait_ge(consts_set, MEMSETS)
            pe.wait_ge(max_in[0], 16)
            for n in range(2):
                scores_chunk(n, n, 0)
                scores_chunk(n, n, 1).then_inc(scores_ready, 1)

            def unit(kind, args, p, u, k):
                if kind == "max":
                    e, b, i = args
                    if i == 0 and b == 0:
                        pe.wait_ge(head_in[e], p * 96 + (96 if e == 1 else 192))
                    chunk_scores(u, k, e, b, i)
                elif kind == "max_row":
                    e, b = args
                    turn_max(u, k, b, p * 4 + {(0, 1): 2, (1, 0): 3, (1, 1): 4, (0, 0): 5}[e, b])
                elif kind == "project":
                    if args == [0, 0]:
                        pe.wait_ge(wp_in, p * 16 + 32)
                    project(u, k, *args)
                elif kind == "value":
                    value(u, k, *args)
                elif kind == "out":
                    pe.wait_ge(aux_free, u - 1)
                    if args[0] == 0:
                        pe.wait_ge(heads_ready, p * 4 + 2)
                        pe.wait_ge(wo_in, p * 16 + 16)
                    cols = slice(args[0] * CH, (args[0] + 1) * CH)
                    nc.tensor.matmul(aux(k), wo[:, :], heads_out[:, cols], start=True, stop=True).then_inc(aux_full, 1)

            def pair(p, units, last):
                base, local = p * U + U0, 0
                for n in range(S):
                    g = p * S + n
                    ahead = not (last and n + 2 >= S)
                    for i in range(max(4, len(units[n]))):
                        if i < 2 and ahead:
                            m = (n + 2) % S
                            if i == 0:
                                if m % T == 0:
                                    e, b = m // HS, m % HS // T
                                    more = 1 if n + 2 >= S else 0
                                    pe.wait_ge(max_in[e], (p + more) * 32 + 16 * (b + 1))
                                pe.wait_ge(probs_ready, g + 1)
                            ins = scores_chunk(g + 2, m, i)
                            if i == 1:
                                ins.then_inc(scores_ready, 1)
                        elif 2 <= i < 4:
                            if i == 2:
                                if n % HS == 0:
                                    pe.wait_ge(v_lo, p * 2 + 1 + n // HS)
                                if n % T == 0:
                                    pe.wait_ge(numer_ready, p * 4 + n // T + 1)
                                pe.wait_ge(lo_ready, g + 1)
                            ins = pv_chunk(n, i - 2)
                            if i == 3:
                                ins.then_inc(pv_done, 1)
                        if i < len(units[n]):
                            kind, *args = units[n][i]
                            unit(kind, args, p, base + local, U0 + local)
                            local += 1

            with pe.Fori(0, PAIRS - 1) as p:
                pair(p, units, False)
            pair(PAIRS - 1, units_last, True)

            def weight(i):
                return ffn[:, i * P:(i + 1) * P]

            pe.wait_ge(const_in, 48)
            pe.wait_ge(probs_ready, PAIRS * S)
            for k in range(3):
                ins = nc.tensor.matmul(bank(CONST)[:, k:k + 1], weight(4 + k), vec[:, 4:5], start=True, stop=True)
            ins.then_inc(gate_const, 1)
            pe.wait_ge(wo_in, 16 * (PAIRS + 1))
            pe.wait_ge(heads_ready, PAIRS * 4 + 2)
            for c in range(4):
                nc.tensor.matmul(bank(OUT + c), wo[:, :], heads_out[:, c * CH:(c + 1) * CH],
                                 start=True, stop=True).then_inc(out_full, 1)
            pe.wait_ge(gate_const_ready, 1)
            for c in range(4):
                pe.wait_ge(attn_ready, c + 1)
                turn4(bank(TURN + c), lambda j: attn[:, (4 * c + j) * P:(4 * c + j + 1) * P]).then_inc(turned, 1)
            for c in range(4):
                pe.wait_ge(norms, 16 + 4 * (c + 1))
                turn4(bank(ZT + c), lambda j: xn[:, 4 * c + j, :]).then_inc(z_turned, 1)
            for c in range(4):
                pe.wait_ge(zT_ready, c + 1)
                for k in range(3):
                    v = GATE + 3 * c + k
                    if v - 8 >= GATE:
                        pe.wait_ge(gates_ready, v - 8 - GATE + 1)
                    elif v - 8 >= ZT:
                        pe.wait_ge(zT_ready, v - 8 - ZT + 1)
                    nc.tensor.matmul(bank(v), weight(k), xnT[:, c * CH:(c + 1) * CH],
                                     start=True, stop=True).then_inc(gate_full, 1)
            for c in range(4):
                pe.wait_ge(gates_ready, HID + c - 8 - GATE + 1)
                nc.tensor.matmul(bank(HID + c), weight(3), xnT[:, c * CH:(c + 1) * CH], start=True, stop=False)
                pe.wait_ge(c_ready, c + 1)
                nc.tensor.matmul(bank(HID + c), weight(7), new_c[:, c * CH:(c + 1) * CH],
                                 start=False, stop=True).then_inc(h_full, 1)
            for c in range(4):
                pe.wait_ge(h_ready, c + 1)
                pe.wait_ge(gates_ready, YT + c - 8 - GATE + 1)
                turn4(bank(YT + c), lambda j: hT[:, (4 * c + j) * P:(4 * c + j + 1) * P]).then_inc(h_turned, 1)


def kernel(**inputs):
    import numpy as np
    import concourse.bacc as bacc
    from concourse.bass_utils import run_bass_kernel_spmd

    a = {k.removeprefix("L0_"): np.asarray(v) for k, v in inputs.items()}
    x = a["attn_x"]
    inner = a["attn_out_w"].shape[1]
    pairs = inner // P
    wT = a["attn_W_w"].T.reshape(P, 3, pairs, P)
    b = a["attn_W_b"].reshape(3, pairs, P)
    w_pair = np.stack([np.concatenate([wT[:, 0, p], wT[:, 1, p], wT[:, 2, p],
                                       np.broadcast_to(b[2, p], (P, P)),
                                       b[0, p][:, None], b[1, p][:, None]], axis=1) for p in range(pairs)])
    arrays = {
        "x": np.ascontiguousarray(x[0]),
        "w_pair": np.ascontiguousarray(w_pair),
        "w_out": np.ascontiguousarray(a["attn_out_w"].T),
        "w_ffn": np.ascontiguousarray(np.concatenate(
            [a["ffn_" + k].T for k in ("wf", "wi", "wc", "wo", "uf", "ui", "uc", "uo")], axis=1)),
        "vecs": np.ascontiguousarray(np.stack(
            [a["ffn_bf"], a["ffn_bi"], a["ffn_bc"], a["ffn_bo"], a["ffn_in_c"], a["attn_out_b"]], axis=1)),
        "ident": np.eye(P, dtype=np.float32),
    }
    nc = bacc.Bacc("TRN2", target_bir_lowering=False, num_devices=1)
    arrays = {f"in_{k}_dram": v for k, v in arrays.items()}
    args = [nc.dram_tensor(k, v.shape, F32, kind="ExternalInput").ap() for k, v in arrays.items()]
    y = nc.dram_tensor("out_dram", x.shape[1:], F32, kind="ExternalOutput").ap()
    bass_attention_then_gated_step(nc, *args, y)
    r = run_bass_kernel_spmd(nc, [arrays], core_ids=[0])
    return r.results[0]["out_dram"].reshape(x.shape)
```

```python
from contextlib import ExitStack

import concourse.bass as bass
from concourse import mybir

F32 = mybir.dt.float32
F32R = mybir.dt.float32r
ACT = mybir.ActivationFunctionType
ALU = mybir.AluOpType
AX = mybir.AxisListType

P = 128
DH = 64
CH = 512
EPS = 1e-5



class Plan:

    def __init__(self, tokens, heads):
        self.tokens = tokens
        self.tiles = tokens // P
        self.qblk = 1024
        self.blocks = tokens // self.qblk
        self.chunks = tokens // CH
        self.pairs = heads // 2
        self.head_steps = self.blocks * self.tiles
        self.steps = 2 * self.head_steps
        self.half = self.tiles // 2 * self.chunks
        self.early = 8
        assert self.blocks == 2 and self.tiles == 16 and self.chunks == 4

    def units(self, last):
        by = [[] for _ in range(self.steps)]
        early, half = self.early, self.half
        for e in range(2):
            s = e * self.head_steps
            here = [("max", e, 1, i) for i in range(early, half)]
            ahead = [("max", 1 - e, 0, i) for i in range(half)]
            begun = [("max", 1 - e, 1, i) for i in range(early)]
            for i, u in enumerate(here):
                by[s + i // 2].append(u)
            by[s + 12].append(("max_row", e, 1))
            if e == 0:
                for c in range(4):
                    by[s + 13 + 2 * c].append(("out", c))
            elif not last:
                for g in range(4):
                    by[s + 13 + g].append(("value", g))
            if e == 0 or not last:
                for i, u in enumerate(ahead):
                    by[s + 12 + i // 2].append(u)
                by[s + 28].append(("max_row", 1 - e, 0))
                for i, u in enumerate(begun):
                    by[s + 28 + i // 2].append(u)
            if e == 0 and not last:
                for i in range(8):
                    by[s + 14 + 2 * i - i // 7].append(("project", i // 4, i % 4))
        return by


    def wavefront(self):
        stages = (("out", 9), ("attn", 8), ("turn", 10), ("attn_moments", 12), ("attn_rstd", 15),
                  ("attn_norm", 14), ("x1", 13), ("z_moments", 12), ("z_rstd", 15), ("z_norm", 11),
                  ("zT", 9), ("z_copy", 6), ("gate_f", 8), ("gate_i", 8), ("gate_g", 8), ("mix", 13),
                  ("c", 8), ("h", 15), ("hT", 10), ("h_moments", 12), ("h_rstd", 15), ("h_norm", 14),
                  ("y", 13))
        begins = (0, 13, 115, 128)
        items = [(begins[0] - 1, 0, "const"), (40, 0, "recips"), (begins[2] - 2, 2, "normalise"),
                 (begins[3] - 2, 3, "normalise")]
        for c, at in enumerate(begins):
            for stage, lasts in stages:
                items.append((at, c, stage))
                at += lasts
        return [(stage, c) for _, c, stage in sorted(items)]


def first_at(units, step):
    return sum(len(s) for s in units[:step])


def last_in(units, kind, *args):
    flat = [u for step in units for u in step]
    return max(i for i, u in enumerate(flat) if u[:1 + len(args)] == (kind,) + args)


def bass_attention_then_gated_step(nc, x, w_pair, w_out, w_ffn, vecs, ident_in, y):
    plan = Plan(x.shape[0], 2 * w_pair.shape[0])
    N, T, QB, PAIRS = plan.tokens, plan.tiles, plan.qblk, plan.pairs
    S, HS = plan.steps, plan.head_steps
    SCALE = float(DH) ** -0.5
    units, units_last = plan.units(False), plan.units(True)
    U = sum(len(s) for s in units)
    HALF, EARLY = plan.half, plan.early
    U0 = 8 + 4 + HALF + 1 + EARLY
    WQ, WK, WV, BV, BQ, BK = 0, P, 2 * P, 3 * P, 4 * P, 4 * P + 1
    assert U % 2 == 0 and (U0 + U) % 2 == U0 % 2
    NSTAT = 6

    with ExitStack() as ctx:
        def sb(name, shape, dt=F32):
            return ctx.enter_context(nc.sbuf_tensor(name, shape, dt))

        def sem(name):
            return ctx.enter_context(nc.semaphore(name))

        staged = sb("staged", [P, 4, N], F32R)
        keys_full = [sb(f"keys_full{e}", [P, N], F32R) for e in range(2)]
        keys_hi = [sb(f"keys_hi{e}", [P, N], F32R) for e in range(2)]
        queries_hi = [sb(f"queries_hi{e}", [P, N], F32R) for e in range(2)]
        queries_lo = [sb(f"queries_lo{e}", [P, N], F32R) for e in range(2)]
        own = [slice(0, DH), slice(DH, P)]
        other = [slice(DH, P), slice(0, DH)]
        max_row_at = [DH, 0]
        values_hi = [sb(f"values_hi{e}", [P, T, 2 * DH], F32R) for e in range(2)]
        values_lo = [sb(f"values_lo{e}", [P, T, DH + 1], F32R) for e in range(2)]
        values_full = sb("values_full", [P, T, P])
        probs = sb("probs", [P, 2, QB])
        probs_hi = sb("probs_hi", [P, 4, QB], F32R)
        probs_lo = sb("probs_lo", [P, 4, QB], F32R)
        numer = sb("numer", [P, QB])
        recip = sb("recip", [P, QB])
        sums = sb("sums", [P, QB // P])
        recips = sb("recips", [P, QB // P])
        heads_out = sb("heads_out", [P, N])
        attn = sb("attn", [P, N])
        xnT = sb("xnT", [P, N])
        wp = sb("wp", [P, w_pair.shape[2]])
        wo = sb("wo", [P, P])
        vec = sb("vec", [P, 6])
        ident = sb("ident", [P, P])
        chunk_max = sb("chunk_max", [P, 2, HALF])
        row_max = sb("row_max", [P, 2, T // 2])
        minus_max = sb("minus_max", [T // 2, P], F32R)
        stats = sb("stats", [P, T, NSTAT])
        moments = sb("moments", [P, T, 2])
        rstd = sb("rstd", [P, T])
        gate_bias = sb("gate_bias", [P, 3])
        var_eps = sb("var_eps", [P, T])
        minus_half = sb("minus_half", [P, 4])

        x_sb = staged[:, 0, :].bitcast(F32).rearrange("p (t d) -> p t d", d=P)
        xn = staged[:, 1, :].bitcast(F32).rearrange("p (t d) -> p t d", d=P)
        y_sb = xn
        hT = staged[:, 2, :].bitcast(F32)
        ffn = staged[:, 3, 0:8 * P].bitcast(F32)
        forget = probs[:, :, :].rearrange("p a c -> p (a c)")
        take = values_full[:, :, :].rearrange("p a c -> p (a c)")
        fresh = heads_out
        new_c = attn
        ps = ctx.enter_context(nc.psum_tensor("ps", [P, 8, CH], F32))
        AUX, PV = 6, 4

        def aux(k):
            return ps[:, AUX + k % 2, :]

        def bank(c, second):
            return ps[:, 2 * c + second, :]

        OUT, TURN, ZT, GATE, HID, YT = 0, 1, 0, (1, 0, 1), 0, 1
        CONST = 7

        x_in = [sem(f"x{c}_in") for c in range(4)]
        x_again_in, ident_in_sem, vec_in = sem("x_again_in"), sem("ident_in"), sem("vec_in")
        wp_in, wo_in, ffn_in = sem("wp_in"), sem("wo_in"), sem("ffn_in")
        head_in = [sem("head0_in"), sem("head1_in")]
        rest_in = [sem("rest0_in"), sem("rest1_in")]
        max_in = [sem("max0_in"), sem("max1_in")]
        first_in = sem("first_in")
        xT_full, xnT_ready = sem("xT_full"), sem("xnT_ready")
        consts_set = sem("consts_set")
        half_set = sem("half_set")
        head_set = [sem("head0_set"), sem("head1_set")]
        xn_ready = sem("xn_ready")
        aux_full, aux_free = sem("aux_full"), sem("aux_free")
        scores_ready = sem("scores_ready")
        probs_ready, hi_ready, lo_ready = sem("probs_ready"), sem("hi_ready"), sem("lo_ready")
        pv_done = sem("pv_done")
        numer_ready = sem("numer_ready")
        sums_in, recips_ready = sem("sums_in"), sem("recips_ready")
        recip_row_in, recip_in = sem("recip_row_in"), sem("recip_in")
        heads_ready = sem("heads_ready")
        stage_hi = sem("stage_hi")
        v_hi, v_lo = sem("v_hi"), sem("v_lo")
        row_max_ready = sem("row_max_ready")
        norm_names = ("x", "attn", "x1", "h")
        stat_done, moments_ready, var_ready, rstd_ready, normed = (
            [sem(f"{what}_{name}") for name in norm_names]
            for what in ("stat_done", "moments_ready", "var_ready", "rstd_ready", "normed"))
        XLN, ALN, ZLN, HLN = range(4)
        gate_const, gate_const_ready = sem("gate_const"), sem("gate_const_ready")
        out_full, attn_ready, turned = sem("out_full"), sem("attn_ready"), sem("turned")
        x1_ready, z_turned, zT_ready = sem("x1_ready"), sem("z_turned"), sem("zT_ready")
        gate_full, gates_ready, mixed, c_ready = sem("gate_full"), sem("gates_ready"), sem("mixed"), sem("c_ready")
        h_full, h_ready, h_turned = sem("h_full"), sem("h_ready"), sem("h_turned")
        y_ready, y_out = sem("y_ready"), sem("y_out")
        PV0 = 4
        HEAD_SETS, MEMSETS = 4, 2

        def st(n):
            b = 2 * (n % 2)
            return ps[:, b:b + 2, :]

        def gates_before(stage, c):
            gates = [item for item in plan.wavefront() if item[0] in ("gate_f", "gate_i", "gate_g")]
            return gates[:gates.index((stage, c))]

        block = ctx.enter_context(nc.Block())

        @block.sync
        def _(sp):
            def copy_rows(e, dst, rows, part):
                done = head_in if dst in (keys_full, queries_hi) else rest_in
                sp.dma_start(dst[e][rows[e], :].bitcast(F32),
                             staged[own[e], part, :].bitcast(F32)).then_inc(done[e], 16)

            def assemble(e):
                for dst, rows, part in ((keys_full, own, 0), (keys_full, other, 1), (keys_hi, own, 0),
                                        (queries_hi, own, 2), (queries_hi, other, 2), (queries_lo, own, 3)):
                    copy_rows(e, dst, rows, part)

            def row_in(e, b, u):
                sp.wait_ge(aux_free, u + 1)
                r = max_row_at[e]
                sp.dma_start(queries_lo[e][r:r + 1, b * QB:(b + 1) * QB].bitcast(F32)
                             .rearrange("a (t q) -> a t q", q=P),
                             minus_max[:, :].bitcast(F32)).then_inc(max_in[e], 16)

            def gather_sums(block):
                sp.wait_ge(numer_ready, block + 2)
                sp.dma_start(sums[:, :], numer[DH:DH + 1, :].rearrange("a (p c) -> a p c", p=P)).then_inc(sums_in, 16)

            def spread_recips(block):
                sp.wait_ge(recips_ready, block + 2)
                sp.dma_start(recip[DH:DH + 1, :].rearrange("a (p c) -> a p c", p=P), recips[:, :]).then_inc(recip_row_in, 16)
                sp.wait_ge(recip_row_in, block * 16 + 32)
                sp.dma_start(recip[0:DH, :], recip[DH:DH + 1, :].unsqueeze(1).to_broadcast([1, DH, QB])).then_inc(recip_in, 16)

            x_tiles, y_tiles = (a.rearrange("(t p) d -> p t d", p=P) for a in (x, y))
            for c in range(4):
                sp.dma_start(x_sb[:, 4 * c:4 * c + 4, :], x_tiles[:, 4 * c:4 * c + 4, :]).then_inc(x_in[c], 16)
                if c == 0:
                    sp.dma_start(ident[:, :], ident_in).then_inc(ident_in_sem, 16)
            sp.dma_start(wp[:, :], w_pair[0]).then_inc(wp_in, 16)
            sp.dma_start(wo[:, :], w_out[0:P, :]).then_inc(wo_in, 16)
            sp.dma_start(vec[:, :], vecs).then_inc(vec_in, 16)
            sp.wait_ge(head_set[0], HEAD_SETS)
            sp.wait_ge(aux_free, 4)
            copy_rows(0, queries_hi, own, 2)
            copy_rows(0, queries_hi, other, 2)
            copy_rows(0, queries_lo, own, 3)
            for c in range(4):
                cols = slice(c * CH, (c + 1) * CH)
                sp.wait_ge(aux_free, 4 + c + 1)
                for part, rows in enumerate((own, other)):
                    sp.dma_start(keys_full[0][rows[0], cols].bitcast(F32),
                                 staged[own[0], part, cols].bitcast(F32)).then_inc(first_in if c < 3 else head_in[0], 16)
            copy_rows(0, keys_hi, own, 0)
            sp.wait_ge(head_set[1], HEAD_SETS)
            row_in(0, 0, U0 - 1 - EARLY)

            def pair(p, units, last):
                base = p * U + U0
                if not last:
                    sp.wait_ge(aux_full, base)
                    sp.dma_start(wp[:, :], w_pair[bass.ds(p + 1, 1)].rearrange("a p n -> (a p) n")
                                 ).then_inc(wp_in, 16)
                gather_sums(p * 4 - 1)
                sp.wait_ge(scores_ready, p * S + 1)
                assemble(1)
                spread_recips(p * 4 - 1)
                if last:
                    for e in range(2):
                        sp.wait_ge(head_in[e], 64 * PAIRS)
                        sp.wait_ge(rest_in[e], 32 * PAIRS)
                    sp.dma_start(ffn, w_ffn).then_inc(ffn_in, 16)
                    sp.dma_start(x_sb, x_tiles).then_inc(x_again_in, 16)
                row_in(0, 1, base + last_in(units, "max_row", 0, 1))
                sp.wait_ge(aux_full, base + last_in(units, "out") + 1)
                sp.dma_start(wo[:, :], w_out[bass.ds(p * P, P), :]).then_inc(wo_in, 16)
                gather_sums(p * 4)
                spread_recips(p * 4)
                row_in(1, 0, base + last_in(units, "max_row", 1, 0))
                if not last:
                    assert first_at(units, HS) >= last_in(units, "project") + 2
                    sp.wait_ge(aux_full, base + first_at(units, HS) + 1)
                    assemble(0)
                gather_sums(p * 4 + 1)
                spread_recips(p * 4 + 1)
                row_in(1, 1, base + last_in(units, "max_row", 1, 1))
                gather_sums(p * 4 + 2)
                spread_recips(p * 4 + 2)
                if not last:
                    row_in(0, 0, base + last_in(units, "max_row", 0, 0))

            with sp.Fori(0, PAIRS - 1) as p:
                pair(p, units, False)
            pair(PAIRS - 1, units_last, True)

            gather_sums(PAIRS * 4 - 1)
            spread_recips(PAIRS * 4 - 1)
            for c in range(4):
                sp.wait_ge(y_ready, c + 1)
                sp.dma_start(y_tiles[:, 4 * c:4 * c + 4, :], xn[:, 4 * c:4 * c + 4, :]).then_inc(y_out, 16)
            sp.wait_ge(y_out, 64)

        @block.gpsimd
        def _(pool):
            def rstd_of(kind, c):
                pool.wait_ge(moments_ready[kind], c + 1)
                nc.gpsimd.tensor_scalar(var_eps[:, 4 * c:4 * c + 4], moments[:, 4 * c:4 * c + 4, 1], EPS, None,
                                        ALU.add).then_inc(var_ready[kind], 1)
                pool.wait_ge(var_ready[kind], c + 1)
                nc.gpsimd.tensor_tensor(rstd[:, 4 * c:4 * c + 4], var_eps[:, 4 * c:4 * c + 4], minus_half[:, :],
                                        ALU.pow).then_inc(rstd_ready[kind], 1)

            def set_operands(e):
                nc.gpsimd.memset(keys_hi[e][:, :].bitcast(F32), 1.0).then_inc(head_set[e], 1)
                nc.gpsimd.memset(queries_lo[e][:, :].bitcast(F32), 0.0).then_inc(head_set[e], 1)

            def set_values(e):
                nc.gpsimd.memset(values_hi[e][:, :, DH:2 * DH].bitcast(F32), 1.0).then_inc(head_set[e], 1)
                nc.gpsimd.memset(values_lo[e][:, :, DH:DH + 1].bitcast(F32), 0.0).then_inc(head_set[e], 1)

            nc.gpsimd.memset(minus_half[:, :], -0.5).then_inc(half_set, 1)
            set_operands(0)
            pool.wait_ge(half_set, 1)
            for c in range(4):
                rstd_of(XLN, c)
            set_values(0)
            nc.gpsimd.memset(probs[:, :, :], 0.0).then_inc(pv_done, PV0)
            nc.gpsimd.memset(attn[:, :], 0.0).then_inc(consts_set, 1)
            nc.gpsimd.memset(numer[0:DH, :], 0.0).then_inc(consts_set, 1)
            nc.gpsimd.memset(heads_out[:, :], 0.0).then_inc(heads_ready, 1)
            set_operands(1)
            set_values(1)

            def value_lo(e, count):
                pool.wait_ge(v_hi, count)
                nc.gpsimd.tensor_tensor(values_lo[e][:, :, 0:DH], values_full[:, :, e * DH:(e + 1) * DH],
                                        values_hi[e][:, :, 0:DH].bitcast(F32), ALU.subtract).then_inc(v_lo, 1)

            def normalise(block, i):
                e, b = i // 2, i % 2
                pool.wait_ge(recip_in, block * 16 + 32)
                pool.wait_ge(heads_ready, block + 2)
                nc.gpsimd.tensor_tensor(heads_out[own[e], b * QB:(b + 1) * QB], numer[0:DH, :],
                                        recip[0:DH, :], ALU.mult).then_inc(heads_ready, 1)

            value_lo(0, 1)

            def pair(p, units, last):
                base = p * U + U0
                pool.wait_ge(heads_ready, p * 4 + 1)
                value_lo(1, p * 2 + 2)
                pool.wait_ge(v_lo, p * 2 + 2)
                normalise(p * 4 - 1, 3)
                pool.wait_ge(aux_full, base + last_in(units, "out") + 1)
                normalise(p * 4, 0)
                normalise(p * 4 + 1, 1)
                if not last:
                    pool.wait_ge(heads_ready, p * 4 + 4)
                    value_lo(0, p * 2 + 3)
                    pool.wait_ge(v_lo, p * 2 + 3)
                normalise(p * 4 + 2, 2)

            with pool.Fori(0, PAIRS - 1) as p:
                pair(p, units, False)
            pair(PAIRS - 1, units_last, True)

            for stage, c in plan.wavefront():
                cols, tiles = slice(c * CH, (c + 1) * CH), slice(4 * c, 4 * c + 4)
                if stage in ("attn_rstd", "z_rstd", "h_rstd"):
                    rstd_of({"attn_rstd": ALN, "z_rstd": ZLN, "h_rstd": HLN}[stage], c)
                elif stage == "x1":
                    pool.wait_ge(x_again_in, 16)
                    pool.wait_ge(normed[ALN], c + 1)
                    nc.gpsimd.tensor_tensor(x_sb[:, tiles, :], x_sb[:, tiles, :], xn[:, tiles, :],
                                            ALU.add).then_inc(x1_ready, 1)
                elif stage == "mix":
                    pool.wait_ge(gates_ready, len(gates_before("gate_g", c)) + 1)
                    nc.gpsimd.tensor_tensor(take[:, cols], take[:, cols], fresh[:, cols],
                                            ALU.mult).then_inc(mixed, 1)
                elif stage == "y":
                    pool.wait_ge(normed[HLN], c + 1)
                    nc.gpsimd.tensor_tensor(y_sb[:, tiles, :], y_sb[:, tiles, :], x_sb[:, tiles, :],
                                            ALU.add).then_inc(y_ready, 1)

        @block.scalar
        def _(act):
            def project_hi(u, k, part, c):
                act.wait_ge(aux_full, u + 1)
                nc.scalar.activation(staged[:, 2 * part, c * CH:(c + 1) * CH], aux(k), ACT.Identity,
                                     bias=wp[:, BQ:BQ + 1] if part else wp[:, BK:BK + 1]).then_inc(stage_hi, 1)

            def exp_step(g, n):
                first = isinstance(g, int) and g < 2
                act.wait_ge(scores_ready, g + 1)
                if first:
                    act.wait_ge(pv_done, PV0)
                else:
                    act.wait_ge(lo_ready, g - 1)
                nc.scalar.activation(probs[:, n % 2, :].rearrange("p (b c) -> p b c", c=CH), st(n),
                                     ACT.Exp, scale=SCALE).then_inc(probs_ready, 1)
                act.wait_ge(probs_ready, g + 1)
                if not first:
                    act.wait_ge(pv_done, PV0 + g - 3)
                nc.scalar.copy(probs_hi[:, n % 4, :], probs[:, n % 2, :]).then_inc(hi_ready, 1)

            def value_hi(e):
                nc.scalar.copy(values_hi[e][:, :, 0:DH], values_full[:, :, e * DH:(e + 1) * DH]).then_inc(v_hi, 1)

            act.wait_ge(wp_in, 16)
            for c in range(4):
                act.wait_ge(xT_full, c + 1)
                nc.scalar.copy(xnT[:, c * CH:(c + 1) * CH], ps[:, c, :]).then_inc(xnT_ready, 1)
                if c > 0:
                    project_hi(c - 1, c - 1, 1, c - 1)
            project_hi(3, 3, 1, 3)
            act.wait_ge(normed[XLN], 4)
            for c in range(4):
                project_hi(4 + c, 4 + c, 0, c)
            act.wait_ge(aux_free, 12)
            value_hi(0)
            exp_step(0, 0)
            exp_step(1, 1)

            def pair(p, units, last):
                for n in range(S):
                    g = p * S + n
                    if n == 2:
                        act.wait_ge(pv_done, PV0 + p * S)
                        value_hi(1)
                    if n == HS + 20 and not last:
                        act.wait_ge(aux_free, p * U + U0 + last_in(units, "value") + 1)
                        act.wait_ge(pv_done, PV0 + p * S + HS)
                        value_hi(0)
                    if not (last and n + 2 >= S):
                        exp_step(g + 2, n + 2)
                    if units[n] and units[n][-1][0] == "project":
                        _, part, c = units[n][-1]
                        if part == 0 and c == 0:
                            for e in range(2):
                                act.wait_ge(head_in[e], p * 64 + 64)
                                act.wait_ge(rest_in[e], p * 32 + 32)
                        u = first_at(units, n + 1) - 1
                        project_hi(p * U + U0 + u, U0 + u, part, c)
                    if n % T == T - 1:
                        act.wait_ge(pv_done, PV0 + g + 1)
                        act.wait_ge(heads_ready, p * 4 + n // T + 2)
                        nc.scalar.copy(numer[0:DH + 1, :].rearrange("p (b c) -> p b c", c=CH),
                                       ps[0:DH + 1, PV:PV + 2, :]).then_inc(numer_ready, 1)

            with act.Fori(0, PAIRS - 1) as p:
                pair(p, units, False)
            pair(PAIRS - 1, units_last, True)

            for stage, c in plan.wavefront():
                cols = slice(c * CH, (c + 1) * CH)
                if stage == "z_copy":
                    act.wait_ge(z_turned, c + 1)
                    nc.scalar.copy(xnT[:, cols], bank(c, ZT)).then_inc(zT_ready, 1)
                elif stage in ("gate_f", "gate_i", "gate_g"):
                    k = ("gate_f", "gate_i", "gate_g").index(stage)
                    act.wait_ge(gate_const_ready, 1)
                    act.wait_ge(gate_full, len(gates_before(stage, c)) + 1)
                    nc.scalar.activation((forget, take, fresh)[k][:, cols], bank(c, GATE[k]),
                                         ACT.Tanh if stage == "gate_g" else ACT.Sigmoid,
                                         bias=gate_bias[:, k:k + 1]).then_inc(gates_ready, 1)
                elif stage == "h":
                    act.wait_ge(h_full, c + 1)
                    nc.scalar.activation(hT[:, cols], bank(c, HID), ACT.Tanh, bias=vec[:, 3:4]).then_inc(h_ready, 1)

        @block.vector
        def _(ve):
            nc.vector.memset(numer[DH:DH + 1, :], 1.0).then_inc(numer_ready, 1)

            def moments_of(kind, c, src):
                for j in range(4):
                    nc.vector.bn_stats(stats[:, 4 * c + j, :], src(j)).then_inc(stat_done[kind], 1)
                ve.wait_ge(stat_done[kind], 4 * (c + 1))
                for j in range(4):
                    ins = nc.vector.bn_aggr(moments[:, 4 * c + j, :], stats[:, 4 * c + j, :])
                ins.then_inc(moments_ready[kind], 1)

            def normalise(kind, c, src):
                ve.wait_ge(rstd_ready[kind], c + 1)
                for j in range(4):
                    t = 4 * c + j
                    ins = nc.vector.tensor_scalar(xn[:, t, :], src(j), moments[:, t, 0:1], rstd[:, t:t + 1],
                                                  ALU.subtract, ALU.mult)
                ins.then_inc(normed[kind], 1)

            for c in range(5):
                if c < 4:
                    ve.wait_ge(x_in[c], 16)
                    moments_of(XLN, c, lambda j: x_sb[:, 4 * c + j, :])
                if c > 0:
                    normalise(XLN, c - 1, lambda j: x_sb[:, 4 * (c - 1) + j, :])

            def project_lo(u, k, part, c, count):
                cols = slice(c * CH, (c + 1) * CH)
                ve.wait_ge(stage_hi, count)
                nc.vector.scalar_tensor_tensor(out=staged[:, 2 * part + 1, cols], in0=aux(k),
                                               scalar=wp[:, BQ:BQ + 1] if part else wp[:, BK:BK + 1],
                                               in1=staged[:, 2 * part, cols].bitcast(F32),
                                               op0=ALU.add, op1=ALU.subtract).then_inc(aux_free, 1)

            def value(u, k, g):
                ve.wait_ge(aux_full, u + 1)
                nc.vector.tensor_tensor(values_full[:, 4 * g:4 * g + 4, :],
                                        aux(k).rearrange("p (t d) -> p t d", d=P),
                                        wp[:, BV:BV + P].unsqueeze(1).to_broadcast([P, 4, P]),
                                        ALU.add).then_inc(aux_free, 1)

            def chunk_of_max(u, k, b, i):
                ve.wait_ge(aux_full, u + 1)
                nc.vector.tensor_reduce(chunk_max[:, b, i:i + 1], aux(k), AX.X, ALU.max).then_inc(aux_free, 1)
                if i == HALF - 1:
                    ve.wait_ge(aux_free, u + 1)
                    nc.vector.tensor_reduce(row_max[:, b, :],
                                            chunk_max[:, b, :].rearrange("p (t c) -> p t c", c=plan.chunks),
                                            AX.X, ALU.max).then_inc(row_max_ready, 1)

            def write_row(u, k):
                ve.wait_ge(aux_full, u + 1)
                nc.vector.tensor_scalar(minus_max[:, :], aux(k)[0:T // 2, 0:P], -1.0, None,
                                        ALU.mult).then_inc(aux_free, 1)

            def lo_step(g, n):
                ve.wait_ge(hi_ready, g + 1)
                if not (isinstance(g, int) and g == 0):
                    ve.wait_ge(pv_done, PV0 + g - 3)
                nc.vector.tensor_tensor(probs_lo[:, n % 4, :], probs[:, n % 2, :],
                                        probs_hi[:, n % 4, :].bitcast(F32), ALU.subtract).then_inc(lo_ready, 1)

            ve.wait_ge(wp_in, 16)
            for i in range(8):
                project_lo(i, i, 1 - i // 4, i % 4, i + 1)
            for g in range(4):
                value(8 + g, 8 + g, g)
            for i in range(HALF):
                chunk_of_max(12 + i, 12 + i, 0, i)
            write_row(12 + HALF, 12 + HALF)
            for i in range(EARLY):
                chunk_of_max(13 + HALF + i, 13 + HALF + i, 1, i)
            lo_step(0, 0)

            def recips_of(block):
                ve.wait_ge(sums_in, block * 16 + 32)
                nc.vector.reciprocal(recips[:, :], sums[:, :]).then_inc(recips_ready, 1)

            def unit(kind, args, p, u, k):
                if kind == "max":
                    e, b, i = args
                    chunk_of_max(u, k, b, i)
                elif kind == "max_row":
                    if args == [0, 1]:
                        ve.wait_ge(max_in[0], p * 32 + 16)
                    elif args == [1, 0]:
                        ve.wait_ge(max_in[0], p * 32 + 32)
                    elif args == [1, 1]:
                        ve.wait_ge(max_in[1], p * 32 + 16)
                    else:
                        ve.wait_ge(max_in[1], p * 32 + 32)
                    write_row(u, k)
                elif kind == "project":
                    part, c = args
                    project_lo(u, k, part, c, p * 8 + 9 + 4 * part + c)
                elif kind == "value":
                    if args[0] == 0:
                        ve.wait_ge(v_hi, p * 2 + 2)
                        ve.wait_ge(v_lo, p * 2 + 2)
                    value(u, k, args[0])
                elif kind == "out":
                    cols = slice(args[0] * CH, (args[0] + 1) * CH)
                    ve.wait_ge(consts_set, MEMSETS)
                    ve.wait_ge(aux_full, u + 1)
                    nc.vector.tensor_tensor(attn[:, cols], aux(k), attn[:, cols], ALU.add).then_inc(aux_free, 1)

            def pair(p, units, last):
                base, local = p * U + U0, 0
                for n in range(S):
                    g = p * S + n
                    if not (last and n + 1 >= S):
                        lo_step(g + 1, n + 1)
                    late = 1 if units[n] and units[n][-1][0] == "project" else 0
                    if n > 0 and units[n - 1] and units[n - 1][-1][0] == "project":
                        unit("project", units[n - 1][-1][1:], p, base + local, U0 + local)
                        local += 1
                    for kind, *args in units[n][:len(units[n]) - late]:
                        unit(kind, args, p, base + local, U0 + local)
                        local += 1
                    if n % T == 4:
                        recips_of(p * 4 + n // T - 1)

            with ve.Fori(0, PAIRS - 1) as p:
                pair(p, units, False)
            pair(PAIRS - 1, units_last, True)

            for stage, c in plan.wavefront():
                cols = slice(c * CH, (c + 1) * CH)

                def turned_tile(j):
                    return bank(c, TURN)[:, j * P:(j + 1) * P]

                if stage == "const":
                    ve.wait_ge(gate_const, 1)
                    nc.vector.tensor_tensor(gate_bias[:, :], ps[:, CONST, 0:3], vec[:, 0:3],
                                            ALU.add).then_inc(gate_const_ready, 1)
                elif stage == "recips":
                    recips_of(PAIRS * 4 - 1)
                elif stage == "normalise":
                    ve.wait_ge(recip_in, PAIRS * 64 + 16)
                    here = slice((c - 2) * CH, (c - 1) * CH)
                    nc.vector.tensor_tensor(heads_out[own[1], cols], numer[0:DH, here], recip[0:DH, here],
                                            ALU.mult).then_inc(heads_ready, 1)
                elif stage == "attn":
                    ve.wait_ge(out_full, c + 1)
                    nc.vector.scalar_tensor_tensor(out=attn[:, cols], in0=bank(c, OUT), scalar=vec[:, 5:6],
                                                   in1=attn[:, cols], op0=ALU.add, op1=ALU.add).then_inc(attn_ready, 1)
                elif stage == "attn_moments":
                    ve.wait_ge(turned, c + 1)
                    moments_of(ALN, c, turned_tile)
                elif stage == "attn_norm":
                    normalise(ALN, c, turned_tile)
                elif stage == "z_moments":
                    ve.wait_ge(x1_ready, c + 1)
                    moments_of(ZLN, c, lambda j: x_sb[:, 4 * c + j, :])
                elif stage == "z_norm":
                    normalise(ZLN, c, lambda j: x_sb[:, 4 * c + j, :])
                elif stage == "c":
                    ve.wait_ge(mixed, c + 1)
                    nc.vector.scalar_tensor_tensor(out=new_c[:, cols], in0=forget[:, cols], scalar=vec[:, 4:5],
                                                   in1=take[:, cols], op0=ALU.mult, op1=ALU.add).then_inc(c_ready, 1)
                elif stage == "h_moments":
                    ve.wait_ge(h_turned, c + 1)
                    moments_of(HLN, c, turned_tile)
                elif stage == "h_norm":
                    normalise(HLN, c, turned_tile)

        @block.tensor
        def _(pe):
            def turn4(dst, src):
                for j in range(4):
                    ins = nc.tensor.transpose(dst[:, j * P:(j + 1) * P], src(j), ident[:, :])
                return ins

            def project(u, k, part, c):
                if not (isinstance(u, int) and u < 2):
                    pe.wait_ge(aux_free, u - 1)
                w = WQ if part else WK
                nc.tensor.matmul(aux(k), wp[:, w:w + P], xnT[:, c * CH:(c + 1) * CH],
                                 start=True, stop=True).then_inc(aux_full, 1)

            def value(u, k, g):
                pe.wait_ge(aux_free, u - 1)
                for j in range(4):
                    t = 4 * g + j
                    ins = nc.tensor.matmul(aux(k)[:, j * P:(j + 1) * P], xnT[:, t * P:(t + 1) * P], wp[:, WV:WV + P],
                                           start=True, stop=True)
                ins.then_inc(aux_full, 1)

            def chunk_scores(u, k, e, b, i):
                t, c = b * (T // 2) + i // plan.chunks, i % plan.chunks
                pe.wait_ge(aux_free, u - 1)
                nc.tensor.matmul(aux(k), queries_hi[e][:, t * P:(t + 1) * P], keys_full[e][:, c * CH:(c + 1) * CH],
                                 start=True, stop=True).then_inc(aux_full, 1)

            def turn_max(u, k, b, count):
                pe.wait_ge(aux_free, u - 1)
                pe.wait_ge(row_max_ready, count)
                nc.tensor.transpose(aux(k)[0:T // 2, 0:P], row_max[:, b, :], ident[:, :]).then_inc(aux_full, 1)

            def scores_chunk(g, n, c):
                hs = n % S
                e, b, jt = hs // HS, hs % HS // T, hs % T
                keys = slice(jt * P, (jt + 1) * P)
                cols = slice(b * QB + c * CH, b * QB + (c + 1) * CH)
                out = ps[:, 2 * (n % 2) + c, :]
                nc.tensor.matmul(out, keys_full[e][:, keys], queries_hi[e][:, cols], start=True, stop=False)
                return nc.tensor.matmul(out, keys_hi[e][:, keys], queries_lo[e][:, cols], start=False, stop=True)

            def pv_chunk(n, c):
                e, jt = n // HS, n % T
                first, final = jt == 0, jt == T - 1
                out = ps[:, PV + c, :]
                hi = probs_hi[:, n % 4, c * CH:(c + 1) * CH]
                nc.tensor.matmul(out, values_hi[e][:, jt, :], hi, start=first, stop=False)
                nc.tensor.matmul(out[0:DH + 1, :], values_lo[e][:, jt, :], hi, start=False, stop=False)
                return nc.tensor.matmul(out, values_hi[e][:, jt, :], probs_lo[:, n % 4, c * CH:(c + 1) * CH],
                                        start=False, stop=final)

            pe.wait_ge(ident_in_sem, 16)
            for c in range(4):
                pe.wait_ge(normed[XLN], c + 1)
                turn4(ps[:, c, :], lambda j: xn[:, 4 * c + j, :]).then_inc(xT_full, 1)
                if c == 1:
                    pe.wait_ge(wp_in, 16)
                if c > 0:
                    pe.wait_ge(xnT_ready, c)
                    project(c - 1, c - 1, 1, c - 1)
            pe.wait_ge(xnT_ready, 4)
            project(3, 3, 1, 3)
            for c in range(4):
                project(4 + c, 4 + c, 0, c)
            for g in range(4):
                value(8 + g, 8 + g, g)
            pe.wait_ge(first_in, 96)
            pe.wait_ge(head_in[0], 64)
            for i in range(HALF):
                chunk_scores(12 + i, 12 + i, 0, 0, i)
            turn_max(12 + HALF, 12 + HALF, 0, 1)
            pe.wait_ge(rest_in[0], 32)
            for i in range(EARLY):
                if i == EARLY // 2:
                    pe.wait_ge(max_in[0], 16)
                    for n in range(2):
                        scores_chunk(n, n, 0)
                        scores_chunk(n, n, 1).then_inc(scores_ready, 1)
                chunk_scores(13 + HALF + i, 13 + HALF + i, 0, 1, i)

            def unit(kind, args, p, u, k):
                if kind == "max":
                    e, b, i = args
                    if i == 0 and b == 0:
                        pe.wait_ge(head_in[e], p * 64 + (64 if e == 1 else 128))
                    chunk_scores(u, k, e, b, i)
                elif kind == "max_row":
                    e, b = args
                    turn_max(u, k, b, p * 4 + {(0, 1): 2, (1, 0): 3, (1, 1): 4, (0, 0): 5}[e, b])
                elif kind == "project":
                    if args == [0, 0]:
                        pe.wait_ge(wp_in, p * 16 + 32)
                    project(u, k, *args)
                elif kind == "value":
                    value(u, k, *args)
                elif kind == "out":
                    pe.wait_ge(aux_free, u - 1)
                    if args[0] == 0:
                        pe.wait_ge(heads_ready, p * 4 + 2)
                        pe.wait_ge(wo_in, p * 16 + 16)
                    cols = slice(args[0] * CH, (args[0] + 1) * CH)
                    nc.tensor.matmul(aux(k), wo[:, :], heads_out[:, cols], start=True, stop=True).then_inc(aux_full, 1)

            def pair(p, units, last):
                base, local = p * U + U0, 0
                for n in range(S):
                    g = p * S + n
                    work = [(u, base + local + i, U0 + local + i) for i, u in enumerate(units[n])]
                    local += len(work)

                    def aux_unit():
                        if work:
                            (kind, *args), u, k = work.pop(0)
                            unit(kind, args, p, u, k)

                    if not (last and n + 2 >= S):
                        m = (n + 2) % S
                        if m % T == 0:
                            e, b = m // HS, m % HS // T
                            if b == 0:
                                pe.wait_ge(rest_in[e], (p + (n + 2) // S) * 32 + 32)
                            pe.wait_ge(max_in[e], (p + (n + 2) // S) * 32 + 16 * (b + 1))
                        pe.wait_ge(probs_ready, g + 1)
                        scores_chunk(g + 2, m, 0)
                        scores_chunk(g + 2, m, 1).then_inc(scores_ready, 1)
                    aux_unit()
                    if n % HS == 0:
                        pe.wait_ge(v_lo, p * 2 + 1 + n // HS)
                    if n % T == 0:
                        pe.wait_ge(numer_ready, p * 4 + n // T + 1)
                    pe.wait_ge(lo_ready, g + 1)
                    pv_chunk(n, 0)
                    aux_unit()
                    pv_chunk(n, 1).then_inc(pv_done, 1)
                    while work:
                        aux_unit()

            with pe.Fori(0, PAIRS - 1) as p:
                pair(p, units, False)
            pair(PAIRS - 1, units_last, True)

            def weight(i):
                return ffn[:, i * P:(i + 1) * P]

            def gate(c, k):
                nc.tensor.matmul(bank(c, GATE[k]), weight(k), xnT[:, c * CH:(c + 1) * CH],
                                 start=True, stop=True).then_inc(gate_full, 1)

            for stage, c in plan.wavefront():
                cols = slice(c * CH, (c + 1) * CH)
                if stage == "const":
                    pe.wait_ge(vec_in, 16)
                    pe.wait_ge(ffn_in, 16)
                    pe.wait_ge(aux_free, (PAIRS - 1) * U + U0 + sum(len(s) for s in units_last))
                    for k in range(3):
                        ins = nc.tensor.matmul(ps[:, CONST, k:k + 1], weight(4 + k), vec[:, 4:5], start=True, stop=True)
                    ins.then_inc(gate_const, 1)
                elif stage == "out":
                    if c == 0:
                        pe.wait_ge(probs_ready, PAIRS * S)
                        pe.wait_ge(wo_in, 16 * (PAIRS + 1))
                        pe.wait_ge(heads_ready, PAIRS * 4 + 1)
                    if c >= 2:
                        pe.wait_ge(heads_ready, PAIRS * 4 + c)
                        pe.wait_ge(numer_ready, PAIRS * 4 + 1)
                    nc.tensor.matmul(bank(c, OUT), wo[:, :], heads_out[:, cols],
                                     start=True, stop=True).then_inc(out_full, 1)
                elif stage == "turn":
                    pe.wait_ge(attn_ready, c + 1)
                    if c == 3:
                        pe.wait_ge(gate_const_ready, 1)
                    turn4(bank(c, TURN), lambda j: attn[:, (4 * c + j) * P:(4 * c + j + 1) * P]).then_inc(turned, 1)
                elif stage == "zT":
                    pe.wait_ge(normed[ZLN], c + 1)
                    turn4(bank(c, ZT), lambda j: xn[:, 4 * c + j, :]).then_inc(z_turned, 1)
                elif stage in ("gate_f", "gate_i", "gate_g"):
                    if stage == "gate_f":
                        pe.wait_ge(zT_ready, c + 1)
                    if stage == "gate_g":
                        pe.wait_ge(gates_ready, len(gates_before("gate_f", c)) + 1)
                    gate(c, ("gate_f", "gate_i", "gate_g").index(stage))
                elif stage == "h":
                    pe.wait_ge(gates_ready, len(gates_before("gate_i", c)) + 1)
                    nc.tensor.matmul(bank(c, HID), weight(3), xnT[:, cols], start=True, stop=False)
                    pe.wait_ge(c_ready, c + 1)
                    nc.tensor.matmul(bank(c, HID), weight(7), new_c[:, cols], start=False, stop=True).then_inc(h_full, 1)
                elif stage == "hT":
                    pe.wait_ge(h_ready, c + 1)
                    pe.wait_ge(gates_ready, len(gates_before("gate_g", c)) + 1)
                    turn4(bank(c, YT), lambda j: hT[:, (4 * c + j) * P:(4 * c + j + 1) * P]).then_inc(h_turned, 1)


def kernel(**inputs):
    import numpy as np
    import concourse.bacc as bacc
    from concourse.bass_utils import run_bass_kernel_spmd

    a = {k.removeprefix("L0_"): np.asarray(v) for k, v in inputs.items()}
    x = a["attn_x"]
    inner = a["attn_out_w"].shape[1]
    pairs = inner // P
    wT = a["attn_W_w"].T.reshape(P, 3, pairs, P)
    b = a["attn_W_b"].reshape(3, pairs, P)
    w_pair = np.stack([np.concatenate([wT[:, 0, p], wT[:, 1, p], wT[:, 2, p],
                                       np.broadcast_to(b[2, p], (P, P)),
                                       b[0, p][:, None], b[1, p][:, None]], axis=1) for p in range(pairs)])
    arrays = {
        "x": np.ascontiguousarray(x[0]),
        "w_pair": np.ascontiguousarray(w_pair),
        "w_out": np.ascontiguousarray(a["attn_out_w"].T),
        "w_ffn": np.ascontiguousarray(np.concatenate(
            [a["ffn_" + k].T for k in ("wf", "wi", "wc", "wo", "uf", "ui", "uc", "uo")], axis=1)),
        "vecs": np.ascontiguousarray(np.stack(
            [a["ffn_bf"], a["ffn_bi"], a["ffn_bc"], a["ffn_bo"], a["ffn_in_c"], a["attn_out_b"]], axis=1)),
        "ident": np.eye(P, dtype=np.float32),
    }
    nc = bacc.Bacc("TRN2", target_bir_lowering=False, num_devices=1)
    arrays = {f"in_{k}_dram": v for k, v in arrays.items()}
    args = [nc.dram_tensor(k, v.shape, F32, kind="ExternalInput").ap() for k, v in arrays.items()]
    y = nc.dram_tensor("out_dram", x.shape[1:], F32, kind="ExternalOutput").ap()
    bass_attention_then_gated_step(nc, *args, y)
    r = run_bass_kernel_spmd(nc, [arrays], core_ids=[0])
    return r.results[0]["out_dram"].reshape(x.shape)
```

```python
from contextlib import ExitStack

import concourse.bass as bass
from concourse import mybir

F32 = mybir.dt.float32
F32R = mybir.dt.float32r
ACT = mybir.ActivationFunctionType
ALU = mybir.AluOpType
AX = mybir.AxisListType

P = 128
DH = 64
CH = 512
EPS = 1e-5



class Plan:

    def __init__(self, tokens, heads):
        self.tokens = tokens
        self.tiles = tokens // P
        self.qblk = 1024
        self.blocks = tokens // self.qblk
        self.chunks = tokens // CH
        self.pairs = heads // 2
        self.head_steps = self.blocks * self.tiles
        self.steps = 2 * self.head_steps
        self.half = self.tiles // 2 * self.chunks
        self.early = 8
        assert self.blocks == 2 and self.tiles == 16 and self.chunks == 4

    def units(self, last):
        by = [[] for _ in range(self.steps)]
        early, half = self.early, self.half
        for e in range(2):
            s = e * self.head_steps
            here = [("max", e, 1, i) for i in range(early, half)]
            ahead = [("max", 1 - e, 0, i) for i in range(half)]
            begun = [("max", 1 - e, 1, i) for i in range(early)]
            for i, u in enumerate(here):
                by[s + i // 2].append(u)
            by[s + 12].append(("max_row", e, 1))
            if e == 0:
                for c in range(4):
                    by[s + 13 + 2 * c].append(("out", c))
            elif not last:
                for g in range(4):
                    by[s + 13 + g].append(("value", g))
            if e == 0 or not last:
                for i, u in enumerate(ahead):
                    by[s + 12 + i // 2].append(u)
                by[s + 28].append(("max_row", 1 - e, 0))
                for i, u in enumerate(begun):
                    by[s + 28 + i // 2].append(u)
            if e == 0 and not last:
                for i in range(8):
                    by[s + 14 + 2 * i - i // 7].append(("project", i // 4, i % 4))
        if last:
            for n, c in self.last_outs.items():
                by[n].append(("last_out", c))
        return by


    def wavefront(self):
        stages = (("out", 9), ("attn", 8), ("attn_moments", 12), ("attn_rstd", 15), ("x1_shifted", 11),
                  ("z_moments", 12), ("z_rstd", 15), ("z_norm", 11), ("zT", 9), ("z_copy", 6),
                  ("gate_i", 8), ("gate_g", 8), ("gate_f", 8), ("h_z", 1), ("mix", 13), ("c", 8), ("x1", 1), ("h", 9),
                  ("h_moments", 12), ("h_rstd", 15), ("h_norm", 14), ("y", 8))
        begins = (-93, -83, 24, 60)
        items = [(-1, 0, "const"), (0, 2, "normalise"), (1, 3, "normalise")]
        for c, at in enumerate(begins):
            for stage, lasts in stages:
                if stage == "h_moments" and c < 2:
                    at = max(at, 120 + 5 * c)
                items.append((at, c, stage))
                at += lasts
        return [(stage, c) for _, c, stage in sorted(items)]

    last_outs = {55: 0, 57: 1}
    in_steps = {55: (("attn_moments", 0),), 57: (("attn_moments", 1),),
                58: (("x1_shifted", 0), ("z_moments", 0)), 60: (("x1_shifted", 1), ("z_moments", 1)),
                61: (("z_norm", 0),), 63: (("z_norm", 1),)}

    def tail(self):
        done = [item for items in self.in_steps.values() for item in items]
        done += [(stage, c) for stage in ("out", "attn") for c in (0, 1)]
        return [item for item in self.wavefront() if item not in done]


def first_at(units, step):
    return sum(len(s) for s in units[:step])


def last_in(units, kind, *args):
    flat = [u for step in units for u in step]
    return max(i for i, u in enumerate(flat) if u[:1 + len(args)] == (kind,) + args)


def bass_attention_then_gated_step(nc, x, w_pair, w_out, w_ffn, vecs, ident_in, y):
    plan = Plan(x.shape[0], 2 * w_pair.shape[0])
    N, T, QB, PAIRS = plan.tokens, plan.tiles, plan.qblk, plan.pairs
    S, HS = plan.steps, plan.head_steps
    SCALE = float(DH) ** -0.5
    units, units_last = plan.units(False), plan.units(True)
    U = sum(len(s) for s in units)
    HALF, EARLY = plan.half, plan.early
    U0 = 8 + 4 + 1 + EARLY
    U_LAST = (PAIRS - 1) * U + U0 + sum(len(s) for s in units_last)
    WQ, WK, WV, BV, BQ, BK = 0, P, 2 * P, 3 * P, 4 * P, 4 * P + 1
    assert U % 2 == 0 and (U0 + U) % 2 == U0 % 2
    NSTAT = 6

    with ExitStack() as ctx:
        def sb(name, shape, dt=F32):
            return ctx.enter_context(nc.sbuf_tensor(name, shape, dt))

        def sem(name):
            return ctx.enter_context(nc.semaphore(name))

        staged = sb("staged", [P, 4, N], F32R)
        keys_full = [sb(f"keys_full{e}", [P, N], F32R) for e in range(2)]
        keys_hi = [sb(f"keys_hi{e}", [P, N], F32R) for e in range(2)]
        queries_hi = [sb(f"queries_hi{e}", [P, N], F32R) for e in range(2)]
        queries_lo = [sb(f"queries_lo{e}", [P, N], F32R) for e in range(2)]
        own = [slice(0, DH), slice(DH, P)]
        other = [slice(DH, P), slice(0, DH)]
        max_row_at = [DH, 0]
        values_hi = [sb(f"values_hi{e}", [P, T, 2 * DH], F32R) for e in range(2)]
        values_lo = [sb(f"values_lo{e}", [P, T, DH + 1], F32R) for e in range(2)]
        values_full = sb("values_full", [P, T, P])
        probs = sb("probs", [P, 2, QB])
        probs_hi = sb("probs_hi", [P, 4, QB], F32R)
        probs_lo = sb("probs_lo", [P, 4, QB], F32R)
        numer = sb("numer", [P, QB])
        recip = sb("recip", [P, QB])
        sums = sb("sums", [P, QB // P])
        recips = sb("recips", [P, QB // P])
        heads_out = sb("heads_out", [P, N])
        attn = sb("attn", [P, N])
        xnT = sb("xnT", [P, N])
        wp = sb("wp", [P, w_pair.shape[2]])
        wo = sb("wo", [P, P])
        vec = sb("vec", [P, vecs.shape[1]])
        ident = sb("ident", [P, P])
        chunk_max = sb("chunk_max", [P, 2, HALF])
        row_max = sb("row_max", [P, 2, T // 2])
        minus_max = sb("minus_max", [T // 2, P], F32R)
        stats = sb("stats", [P, T, NSTAT])
        moments = sb("moments", [P, T, 2])
        rstd = sb("rstd", [P, T])
        attn_moments = sb("attn_moments", [P, T, 2])
        attn_rstd = sb("attn_rstd", [P, T])
        attn_shift = sb("attn_shift", [P, T])
        gate_bias = sb("gate_bias", [P, 3])
        var_eps = sb("var_eps", [P, T])
        minus_half = sb("minus_half", [P, 4])

        x_sb = staged[:, 0, :].bitcast(F32).rearrange("p (t d) -> p t d", d=P)
        xn = staged[:, 1, :].bitcast(F32).rearrange("p (t d) -> p t d", d=P)
        y_sb = xn
        h_sb = staged[:, 2, :].bitcast(F32)
        ffn = staged[:, 3, 0:w_ffn.shape[1]].bitcast(F32)
        bo_row, ones_row = ffn[0:1, 8 * P:8 * P + CH], ffn[0:1, 8 * P + CH:8 * P + CH + P]
        forget = probs[:, :, :].rearrange("p a c -> p (a c)")
        take = values_full[:, :, :].rearrange("p a c -> p (a c)")
        fresh = heads_out
        new_c = attn

        ps = ctx.enter_context(nc.psum_tensor("ps", [P, 8, CH], F32))
        AUX, PV = 6, 4

        def aux(k):
            return ps[:, AUX + k % 2, :]

        def first_banks(i):
            return ps[:, i % 3 * 2:i % 3 * 2 + 2, :]

        def bank(c, second):
            return ps[:, 2 * c + second, :]

        OUT, ZT, GATE, HID = 0, 1, (0, 0, 1), 1
        CONST = 7

        x_in = [sem(f"x{c}_in") for c in range(4)]
        x_again_in, ident_in_sem, vec_in = sem("x_again_in"), sem("ident_in"), sem("vec_in")
        wp_in, wo_in, ffn_in = sem("wp_in"), sem("wo_in"), sem("ffn_in")
        head_in = [sem("head0_in"), sem("head1_in")]
        rest_in = [sem("rest0_in"), sem("rest1_in")]
        max_in = [sem("max0_in"), sem("max1_in")]
        first_in = sem("first_in")
        first_full, first_free = sem("first_full"), sem("first_free")
        xT_full, xnT_ready = sem("xT_full"), sem("xnT_ready")
        half_set = sem("half_set")
        head_set = [sem("head0_set"), sem("head1_set")]
        consts_set = sem("consts_set")
        aux_full, aux_free = sem("aux_full"), sem("aux_free")
        scores_ready = sem("scores_ready")
        probs_ready, hi_ready, lo_ready = sem("probs_ready"), sem("hi_ready"), sem("lo_ready")
        pv_done = sem("pv_done")
        half_done, half_out = sem("half_done"), sem("half_out")
        numer_ready = sem("numer_ready")
        sums_in, recips_ready = sem("sums_in"), sem("recips_ready")
        recip_row_in, recip_in = sem("recip_row_in"), sem("recip_in")
        heads_ready = sem("heads_ready")
        stage_hi = sem("stage_hi")
        v_hi, v_lo = sem("v_hi"), sem("v_lo")
        row_max_ready = sem("row_max_ready")
        norm_names = ("x", "attn", "x1", "h")
        stat_done, moments_ready, var_ready, rstd_ready, normed = (
            [sem(f"{what}_{name}") for name in norm_names]
            for what in ("stat_done", "moments_ready", "var_ready", "rstd_ready", "normed"))
        XLN, ALN, ZLN, HLN = range(4)
        gate_const, gate_const_ready = sem("gate_const"), sem("gate_const_ready")
        out_full, attn_ready, x1_shifted = sem("out_full"), sem("attn_ready"), sem("x1_shifted")
        shift_ready = sem("shift_ready")
        x1_ready, z_turned, zT_ready = sem("x1_ready"), sem("z_turned"), sem("zT_ready")
        gate_full, gates_ready, mixed, c_ready = sem("gate_full"), sem("gates_ready"), sem("mixed"), sem("c_ready")
        h_full, h_ready = sem("h_full"), sem("h_ready")
        y_ready, y_out = sem("y_ready"), sem("y_out")
        PV0 = 4
        HEAD_SETS, MEMSETS = 4, 2

        def st(n):
            b = 2 * (n % 2)
            return ps[:, b:b + 2, :]

        def gates_before(stage, c):
            gates = [item for item in plan.wavefront() if item[0] in ("gate_f", "gate_i", "gate_g")]
            return gates[:gates.index((stage, c))]

        block = ctx.enter_context(nc.Block())

        @block.sync
        def _(sp):
            def copy_rows(e, dst, rows, part):
                done = head_in if dst in (keys_full, queries_hi) else rest_in
                sp.dma_start(dst[e][rows[e], :].bitcast(F32),
                             staged[own[e], part, :].bitcast(F32)).then_inc(done[e], 16)

            def assemble(e):
                for dst, rows, part in ((keys_full, own, 0), (keys_full, other, 1), (keys_hi, own, 0),
                                        (queries_hi, own, 2), (queries_hi, other, 2), (queries_lo, own, 3)):
                    copy_rows(e, dst, rows, part)

            def row_in(e, b, u):
                sp.wait_ge(aux_free, u + 1)
                r = max_row_at[e]
                sp.dma_start(queries_lo[e][r:r + 1, b * QB:(b + 1) * QB].bitcast(F32)
                             .rearrange("a (t q) -> a t q", q=P),
                             minus_max[:, :].bitcast(F32)).then_inc(max_in[e], 16)

            def gather_sums(block):
                sp.wait_ge(numer_ready, block + 2)
                sp.dma_start(sums[:, :], numer[DH:DH + 1, :].rearrange("a (p c) -> a p c", p=P)).then_inc(sums_in, 16)

            def spread_recips(block):
                sp.wait_ge(recips_ready, block + 2)
                sp.dma_start(recip[DH:DH + 1, :].rearrange("a (p c) -> a p c", p=P), recips[:, :]).then_inc(recip_row_in, 16)
                sp.wait_ge(recip_row_in, block * 16 + 32)
                sp.dma_start(recip[0:DH, :], recip[DH:DH + 1, :].unsqueeze(1).to_broadcast([1, DH, QB])).then_inc(recip_in, 16)

            x_tiles, y_tiles = (a.rearrange("(t p) d -> p t d", p=P) for a in (x, y))
            for c in range(4):
                sp.dma_start(x_sb[:, 4 * c:4 * c + 4, :], x_tiles[:, 4 * c:4 * c + 4, :]).then_inc(x_in[c], 16)
                if c == 0:
                    sp.dma_start(ident[:, :], ident_in).then_inc(ident_in_sem, 16)
            sp.dma_start(wp[:, :], w_pair[0]).then_inc(wp_in, 16)
            sp.dma_start(wo[:, :], w_out[0:P, :]).then_inc(wo_in, 16)
            sp.dma_start(vec[:, :], vecs).then_inc(vec_in, 16)
            sp.wait_ge(head_set[0], HEAD_SETS)
            sp.wait_ge(aux_free, 4)
            copy_rows(0, queries_hi, own, 2)
            copy_rows(0, queries_hi, other, 2)
            copy_rows(0, queries_lo, own, 3)
            for c in range(4):
                cols = slice(c * CH, (c + 1) * CH)
                sp.wait_ge(aux_free, 4 + c + 1)
                for part, rows in enumerate((own, other)):
                    sp.dma_start(keys_full[0][rows[0], cols].bitcast(F32),
                                 staged[own[0], part, cols].bitcast(F32)).then_inc(first_in if c < 3 else head_in[0], 16)
            copy_rows(0, keys_hi, own, 0)
            sp.wait_ge(head_set[1], HEAD_SETS)
            row_in(0, 0, U0 - 1 - EARLY)

            def pair(p, units, last):
                base = p * U + U0
                if not last:
                    sp.wait_ge(aux_full, base)
                    sp.dma_start(wp[:, :], w_pair[bass.ds(p + 1, 1)].rearrange("a p n -> (a p) n")
                                 ).then_inc(wp_in, 16)
                gather_sums(p * 4 - 1)
                sp.wait_ge(scores_ready, p * S + 1)
                assemble(1)
                spread_recips(p * 4 - 1)
                if last:
                    for e in range(2):
                        sp.wait_ge(head_in[e], 64 * PAIRS)
                        sp.wait_ge(rest_in[e], 32 * PAIRS)
                    sp.dma_start(ffn, w_ffn).then_inc(ffn_in, 16)
                    sp.dma_start(x_sb, x_tiles).then_inc(x_again_in, 16)
                row_in(0, 1, base + last_in(units, "max_row", 0, 1))
                sp.wait_ge(aux_full, base + last_in(units, "out") + 1)
                sp.dma_start(wo[:, :], w_out[bass.ds(p * P, P), :]).then_inc(wo_in, 16)
                gather_sums(p * 4)
                spread_recips(p * 4)
                row_in(1, 0, base + last_in(units, "max_row", 1, 0))
                if not last:
                    assert first_at(units, HS) >= last_in(units, "project") + 2
                    sp.wait_ge(aux_full, base + first_at(units, HS) + 1)
                    assemble(0)
                gather_sums(p * 4 + 1)
                spread_recips(p * 4 + 1)
                row_in(1, 1, base + last_in(units, "max_row", 1, 1))
                gather_sums(p * 4 + 2)
                spread_recips(p * 4 + 2)
                if not last:
                    row_in(0, 0, base + last_in(units, "max_row", 0, 0))

            with sp.Fori(0, PAIRS - 1) as p:
                pair(p, units, False)
            pair(PAIRS - 1, units_last, True)

            for c in range(4):
                sp.wait_ge(y_ready, c + 1)
                sp.dma_start(y_tiles[:, 4 * c:4 * c + 4, :], xn[:, 4 * c:4 * c + 4, :]).then_inc(y_out, 16)
            sp.wait_ge(y_out, 64)

        @block.gpsimd
        def _(pool):
            def rstd_of(kind, c):
                of, to = (attn_moments, attn_rstd) if kind == ALN else (moments, rstd)
                pool.wait_ge(moments_ready[kind], c + 1)
                nc.gpsimd.tensor_scalar(var_eps[:, 4 * c:4 * c + 4], of[:, 4 * c:4 * c + 4, 1], EPS, None,
                                        ALU.add).then_inc(var_ready[kind], 1)
                pool.wait_ge(var_ready[kind], c + 1)
                nc.gpsimd.tensor_tensor(to[:, 4 * c:4 * c + 4], var_eps[:, 4 * c:4 * c + 4], minus_half[:, :],
                                        ALU.pow).then_inc(rstd_ready[kind], 1)

            def set_operands(e):
                nc.gpsimd.memset(keys_hi[e][:, :].bitcast(F32), 1.0).then_inc(head_set[e], 1)
                nc.gpsimd.memset(queries_lo[e][:, :].bitcast(F32), 0.0).then_inc(head_set[e], 1)

            def set_values(e):
                nc.gpsimd.memset(values_hi[e][:, :, DH:2 * DH].bitcast(F32), 1.0).then_inc(head_set[e], 1)
                nc.gpsimd.memset(values_lo[e][:, :, DH:DH + 1].bitcast(F32), 0.0).then_inc(head_set[e], 1)

            nc.gpsimd.memset(minus_half[:, :], -0.5).then_inc(half_set, 1)
            set_operands(0)
            pool.wait_ge(half_set, 1)
            for c in range(4):
                rstd_of(XLN, c)
            set_values(0)
            nc.gpsimd.memset(probs[:, :, :], 0.0).then_inc(pv_done, PV0)
            pool.wait_ge(vec_in, 16)
            nc.gpsimd.tensor_copy(attn[:, :].rearrange("p (t d) -> p t d", d=P),
                                  vec[:, 4:4 + P].unsqueeze(1).to_broadcast([P, T, P])).then_inc(consts_set, 1)
            nc.gpsimd.memset(numer[0:DH, :], 0.0).then_inc(consts_set, 1)
            nc.gpsimd.memset(heads_out[:, :], 0.0).then_inc(heads_ready, 1)
            set_operands(1)
            set_values(1)

            def value_lo(e, count):
                pool.wait_ge(v_hi, count)
                nc.gpsimd.tensor_tensor(values_lo[e][:, :, 0:DH], values_full[:, :, e * DH:(e + 1) * DH],
                                        values_hi[e][:, :, 0:DH].bitcast(F32), ALU.subtract).then_inc(v_lo, 1)

            def normalise(block, i):
                e, b = i // 2, i % 2
                pool.wait_ge(recip_in, block * 16 + 32)
                pool.wait_ge(heads_ready, block + 2)
                nc.gpsimd.tensor_tensor(heads_out[own[e], b * QB:(b + 1) * QB], numer[0:DH, :],
                                        recip[0:DH, :], ALU.mult).then_inc(heads_ready, 1)

            value_lo(0, 1)

            def pair(p, units, last):
                base = p * U + U0
                pool.wait_ge(heads_ready, p * 4 + 1)
                value_lo(1, p * 2 + 2)
                pool.wait_ge(v_lo, p * 2 + 2)
                normalise(p * 4 - 1, 3)
                pool.wait_ge(aux_full, base + last_in(units, "out") + 1)
                normalise(p * 4, 0)
                normalise(p * 4 + 1, 1)
                if not last:
                    pool.wait_ge(heads_ready, p * 4 + 4)
                    value_lo(0, p * 2 + 3)
                    pool.wait_ge(v_lo, p * 2 + 3)
                normalise(p * 4 + 2, 2)

            with pool.Fori(0, PAIRS - 1) as p:
                pair(p, units, False)
            pair(PAIRS - 1, units_last, True)

            for stage, c in plan.wavefront():
                cols, tiles = slice(c * CH, (c + 1) * CH), slice(4 * c, 4 * c + 4)
                if stage in ("attn_rstd", "z_rstd", "h_rstd"):
                    rstd_of({"attn_rstd": ALN, "z_rstd": ZLN, "h_rstd": HLN}[stage], c)
                elif stage == "x1":
                    pool.wait_ge(rstd_ready[ALN], c + 1)
                    nc.gpsimd.tensor_tensor(attn_shift[:, tiles], attn_moments[:, tiles, 0], attn_rstd[:, tiles],
                                            ALU.mult).then_inc(shift_ready, 1)
                    pool.wait_ge(shift_ready, c + 1)
                    pool.wait_ge(normed[ZLN], c + 1)
                    nc.gpsimd.tensor_tensor(x_sb[:, tiles, :], x_sb[:, tiles, :],
                                            attn_shift[:, tiles].unsqueeze(2).to_broadcast([P, 4, P]),
                                            ALU.subtract).then_inc(x1_ready, 1)
                elif stage == "mix":
                    pool.wait_ge(gates_ready, len(gates_before("gate_g", c)) + 1)
                    nc.gpsimd.tensor_tensor(take[:, cols], take[:, cols], fresh[:, cols],
                                            ALU.mult).then_inc(mixed, 1)

        @block.scalar
        def _(act):
            def project_hi(u, k, part, c):
                act.wait_ge(aux_full, u + 1)
                nc.scalar.activation(staged[:, 2 * part, c * CH:(c + 1) * CH], aux(k), ACT.Identity,
                                     bias=wp[:, BQ:BQ + 1] if part else wp[:, BK:BK + 1]).then_inc(stage_hi, 1)

            def exp_step(g, n):
                first = isinstance(g, int) and g < 2
                act.wait_ge(scores_ready, g + 1)
                if first:
                    act.wait_ge(pv_done, PV0)
                else:
                    act.wait_ge(lo_ready, g - 1)
                nc.scalar.activation(probs[:, n % 2, :].rearrange("p (b c) -> p b c", c=CH), st(n),
                                     ACT.Exp, scale=SCALE).then_inc(probs_ready, 1)
                act.wait_ge(probs_ready, g + 1)
                if not first:
                    act.wait_ge(pv_done, PV0 + g - 3)
                nc.scalar.copy(probs_hi[:, n % 4, :], probs[:, n % 2, :]).then_inc(hi_ready, 1)

            def value_hi(e):
                nc.scalar.copy(values_hi[e][:, :, 0:DH], values_full[:, :, e * DH:(e + 1) * DH]).then_inc(v_hi, 1)

            act.wait_ge(wp_in, 16)
            for c in range(4):
                act.wait_ge(xT_full, c + 1)
                nc.scalar.copy(xnT[:, c * CH:(c + 1) * CH], ps[:, c, :]).then_inc(xnT_ready, 1)
                if c > 0:
                    project_hi(c - 1, c - 1, 1, c - 1)
            project_hi(3, 3, 1, 3)
            act.wait_ge(normed[XLN], 4)
            for c in range(4):
                project_hi(4 + c, 4 + c, 0, c)
            act.wait_ge(aux_free, 12)
            value_hi(0)
            exp_step(0, 0)
            exp_step(1, 1)

            def pair(p, units, last):
                for n in range(S):
                    g = p * S + n
                    if n == 2:
                        act.wait_ge(pv_done, PV0 + p * S)
                        value_hi(1)
                    if n == HS + 20 and not last:
                        act.wait_ge(aux_free, p * U + U0 + last_in(units, "value") + 1)
                        act.wait_ge(pv_done, PV0 + p * S + HS)
                        value_hi(0)
                    if not (last and n + 2 >= S):
                        exp_step(g + 2, n + 2)
                    if units[n] and units[n][-1][0] == "project":
                        _, part, c = units[n][-1]
                        if part == 0 and c == 0:
                            for e in range(2):
                                act.wait_ge(head_in[e], p * 64 + 64)
                                act.wait_ge(rest_in[e], p * 32 + 32)
                        u = first_at(units, n + 1) - 1
                        project_hi(p * U + U0 + u, U0 + u, part, c)
                    if n % T == T - 1 and not (last and n == S - 1):
                        act.wait_ge(half_done, p * 4 + n // T + 1)
                        act.wait_ge(heads_ready, p * 4 + n // T + 2)
                        nc.scalar.copy(numer[0:DH + 1, 0:CH], ps[0:DH + 1, PV, :]).then_inc(half_out, 1)
                        act.wait_ge(pv_done, PV0 + g + 1)
                        nc.scalar.copy(numer[0:DH + 1, CH:QB], ps[0:DH + 1, PV + 1, :]).then_inc(numer_ready, 1)

            with act.Fori(0, PAIRS - 1) as p:
                pair(p, units, False)
            pair(PAIRS - 1, units_last, True)

            for stage, c in plan.wavefront():
                cols = slice(c * CH, (c + 1) * CH)
                if stage == "z_copy":
                    act.wait_ge(z_turned, c + 1)
                    nc.scalar.copy(xnT[:, cols], bank(c, ZT)).then_inc(zT_ready, 1)
                elif stage in ("gate_f", "gate_i", "gate_g"):
                    k = ("gate_f", "gate_i", "gate_g").index(stage)
                    act.wait_ge(gate_const_ready, 1)
                    act.wait_ge(gate_full, len(gates_before(stage, c)) + 1)
                    nc.scalar.activation((forget, take, fresh)[k][:, cols], bank(c, GATE[k]),
                                         ACT.Tanh if stage == "gate_g" else ACT.Sigmoid,
                                         bias=gate_bias[:, k:k + 1]).then_inc(gates_ready, 1)
                elif stage == "h":
                    act.wait_ge(h_full, c + 1)
                    nc.scalar.activation(h_sb[:, cols], bank(c, HID), ACT.Tanh).then_inc(h_ready, 1)

        @block.vector
        def _(ve):
            nc.vector.memset(numer[DH:DH + 1, 0:CH], 1.0).then_inc(half_out, 1)
            nc.vector.memset(numer[DH:DH + 1, CH:QB], 1.0).then_inc(numer_ready, 1)

            def moments_of(kind, c, src):
                for j in range(4):
                    nc.vector.bn_stats(stats[:, 4 * c + j, :], src(j)).then_inc(stat_done[kind], 1)
                ve.wait_ge(stat_done[kind], 4 * (c + 1))
                to = attn_moments if kind == ALN else moments
                for j in range(4):
                    ins = nc.vector.bn_aggr(to[:, 4 * c + j, :], stats[:, 4 * c + j, :])
                ins.then_inc(moments_ready[kind], 1)

            def normalise(kind, c, src):
                ve.wait_ge(rstd_ready[kind], c + 1)
                for j in range(4):
                    t = 4 * c + j
                    ins = nc.vector.tensor_scalar(xn[:, t, :], src(j), moments[:, t, 0:1], rstd[:, t:t + 1],
                                                  ALU.subtract, ALU.mult)
                ins.then_inc(normed[kind], 1)

            for c in range(5):
                if c < 4:
                    ve.wait_ge(x_in[c], 16)
                    moments_of(XLN, c, lambda j: x_sb[:, 4 * c + j, :])
                if c > 0:
                    normalise(XLN, c - 1, lambda j: x_sb[:, 4 * (c - 1) + j, :])

            def project_lo(u, k, part, c, count):
                cols = slice(c * CH, (c + 1) * CH)
                ve.wait_ge(stage_hi, count)
                nc.vector.scalar_tensor_tensor(out=staged[:, 2 * part + 1, cols], in0=aux(k),
                                               scalar=wp[:, BQ:BQ + 1] if part else wp[:, BK:BK + 1],
                                               in1=staged[:, 2 * part, cols].bitcast(F32),
                                               op0=ALU.add, op1=ALU.subtract).then_inc(aux_free, 1)

            def value(u, k, g):
                ve.wait_ge(aux_full, u + 1)
                nc.vector.tensor_tensor(values_full[:, 4 * g:4 * g + 4, :],
                                        aux(k).rearrange("p (t d) -> p t d", d=P),
                                        wp[:, BV:BV + P].unsqueeze(1).to_broadcast([P, 4, P]),
                                        ALU.add).then_inc(aux_free, 1)

            def chunk_of_max(u, k, b, i):
                ve.wait_ge(aux_full, u + 1)
                nc.vector.tensor_reduce(chunk_max[:, b, i:i + 1], aux(k), AX.X, ALU.max).then_inc(aux_free, 1)
                if i == HALF - 1:
                    ve.wait_ge(aux_free, u + 1)
                    nc.vector.tensor_reduce(row_max[:, b, :],
                                            chunk_max[:, b, :].rearrange("p (t c) -> p t c", c=plan.chunks),
                                            AX.X, ALU.max).then_inc(row_max_ready, 1)

            def write_row(u, k):
                ve.wait_ge(aux_full, u + 1)
                nc.vector.tensor_scalar(minus_max[:, :], aux(k)[0:T // 2, 0:P], -1.0, None,
                                        ALU.mult).then_inc(aux_free, 1)

            def lo_step(g, n):
                ve.wait_ge(hi_ready, g + 1)
                if not (isinstance(g, int) and g == 0):
                    ve.wait_ge(pv_done, PV0 + g - 3)
                nc.vector.tensor_tensor(probs_lo[:, n % 4, :], probs[:, n % 2, :],
                                        probs_hi[:, n % 4, :].bitcast(F32), ALU.subtract).then_inc(lo_ready, 1)

            ve.wait_ge(wp_in, 16)
            for i in range(8):
                project_lo(i, i, 1 - i // 4, i % 4, i + 1)
            for g in range(4):
                value(8 + g, 8 + g, g)
            for i in range(HALF // 2):
                ve.wait_ge(first_full, i + 1)
                nc.vector.tensor_reduce(chunk_max[:, 0, i:i + 1],
                                        first_banks(i).rearrange("p b c -> p (b c)"), AX.X, ALU.max).then_inc(first_free, 1)
            ve.wait_ge(first_free, HALF // 2)
            nc.vector.tensor_reduce(row_max[:, 0, :],
                                    chunk_max[:, 0, 0:HALF // 2].rearrange("p (t c) -> p t c", c=plan.chunks // 2),
                                    AX.X, ALU.max).then_inc(row_max_ready, 1)
            write_row(12, 12)
            for i in range(EARLY):
                chunk_of_max(13 + i, 13 + i, 1, i)
            lo_step(0, 0)

            def recips_of(block):
                ve.wait_ge(sums_in, block * 16 + 32)
                nc.vector.reciprocal(recips[:, :], sums[:, :]).then_inc(recips_ready, 1)

            def unit(kind, args, p, u, k):
                if kind == "max":
                    e, b, i = args
                    chunk_of_max(u, k, b, i)
                elif kind == "max_row":
                    if args == [0, 1]:
                        ve.wait_ge(max_in[0], p * 32 + 16)
                    elif args == [1, 0]:
                        ve.wait_ge(max_in[0], p * 32 + 32)
                    elif args == [1, 1]:
                        ve.wait_ge(max_in[1], p * 32 + 16)
                    else:
                        ve.wait_ge(max_in[1], p * 32 + 32)
                    write_row(u, k)
                elif kind == "project":
                    part, c = args
                    project_lo(u, k, part, c, p * 8 + 9 + 4 * part + c)
                elif kind == "value":
                    if args[0] == 0:
                        ve.wait_ge(v_hi, p * 2 + 2)
                        ve.wait_ge(v_lo, p * 2 + 2)
                    value(u, k, args[0])
                elif kind in ("out", "last_out"):
                    cols = slice(args[0] * CH, (args[0] + 1) * CH)
                    ve.wait_ge(consts_set, MEMSETS)
                    ve.wait_ge(aux_full, u + 1)
                    nc.vector.tensor_tensor(attn[:, cols], aux(k), attn[:, cols], ALU.add).then_inc(aux_free, 1)

            def after_attention(stage, c):
                cols, tiles = slice(c * CH, (c + 1) * CH), slice(4 * c, 4 * c + 4)
                if stage == "const":
                    ve.wait_ge(gate_const, 1)
                    nc.vector.tensor_tensor(gate_bias[:, :], ps[:, CONST, 0:3], vec[:, 0:3],
                                            ALU.add).then_inc(gate_const_ready, 1)
                elif stage == "normalise":
                    here, at = slice((c - 2) * CH, (c - 1) * CH), PV + c - 2
                    if c == 2:
                        ve.wait_ge(half_done, PAIRS * 4)
                        ve.wait_ge(heads_ready, PAIRS * 4 + 1)
                    else:
                        ve.wait_ge(pv_done, PV0 + PAIRS * S)
                    nc.vector.reciprocal(recip[0:DH, here], ps[DH:P, at, :]).then_inc(recips_ready, 1)
                    ve.wait_ge(recips_ready, PAIRS * 4 + c - 1)
                    nc.vector.tensor_tensor(heads_out[own[1], cols], ps[0:DH, at, :], recip[0:DH, here],
                                            ALU.mult).then_inc(heads_ready, 1)
                elif stage == "attn":
                    ve.wait_ge(out_full, c - 1)
                    nc.vector.tensor_tensor(attn[:, cols], bank(c, OUT), attn[:, cols], ALU.add).then_inc(attn_ready, 1)
                elif stage == "attn_moments":
                    if c < 2:
                        ve.wait_ge(aux_free, U_LAST - 1 + c)
                    else:
                        ve.wait_ge(attn_ready, c - 1)
                    moments_of(ALN, c, lambda j: attn[:, (4 * c + j) * P:(4 * c + j + 1) * P])
                elif stage == "x1_shifted":
                    ve.wait_ge(x_again_in, 16)
                    ve.wait_ge(rstd_ready[ALN], c + 1)
                    for t in range(4 * c, 4 * c + 4):
                        nc.vector.scalar_tensor_tensor(out=x_sb[:, t, :], in0=attn[:, t * P:(t + 1) * P],
                                                       scalar=attn_rstd[:, t:t + 1], in1=x_sb[:, t, :],
                                                       op0=ALU.mult, op1=ALU.add).then_inc(x1_shifted, 1)
                elif stage == "z_moments":
                    ve.wait_ge(x1_shifted, 4 * (c + 1))
                    moments_of(ZLN, c, lambda j: x_sb[:, 4 * c + j, :])
                elif stage == "z_norm":
                    normalise(ZLN, c, lambda j: x_sb[:, 4 * c + j, :])
                elif stage == "c":
                    ve.wait_ge(mixed, c + 1)
                    ve.wait_ge(gates_ready, len(gates_before("gate_f", c)) + 1)
                    nc.vector.scalar_tensor_tensor(out=new_c[:, cols], in0=forget[:, cols], scalar=vec[:, 3:4],
                                                   in1=take[:, cols], op0=ALU.mult, op1=ALU.add).then_inc(c_ready, 1)
                elif stage == "h_moments":
                    ve.wait_ge(h_ready, c + 1)
                    moments_of(HLN, c, lambda j: h_sb[:, (4 * c + j) * P:(4 * c + j + 1) * P])
                elif stage == "h_norm":
                    normalise(HLN, c, lambda j: h_sb[:, (4 * c + j) * P:(4 * c + j + 1) * P])
                elif stage == "y":
                    ve.wait_ge(normed[HLN], c + 1)
                    ve.wait_ge(x1_ready, c + 1)
                    nc.vector.tensor_tensor(y_sb[:, tiles, :], y_sb[:, tiles, :], x_sb[:, tiles, :],
                                            ALU.add).then_inc(y_ready, 1)

            def pair(p, units, last):
                base, local = p * U + U0, 0
                for n in range(S):
                    g = p * S + n
                    if not (last and n + 1 >= S):
                        lo_step(g + 1, n + 1)
                    late = 1 if units[n] and units[n][-1][0] == "project" else 0
                    if n > 0 and units[n - 1] and units[n - 1][-1][0] == "project":
                        unit("project", units[n - 1][-1][1:], p, base + local, U0 + local)
                        local += 1
                    for kind, *args in units[n][:len(units[n]) - late]:
                        unit(kind, args, p, base + local, U0 + local)
                        local += 1
                    if n % T == (2 if last and n > S - T else 4):
                        recips_of(p * 4 + n // T - 1)
                    if last:
                        for stage, c in plan.in_steps.get(n, ()):
                            after_attention(stage, c)

            with ve.Fori(0, PAIRS - 1) as p:
                pair(p, units, False)
            pair(PAIRS - 1, units_last, True)

            for stage, c in plan.tail():
                after_attention(stage, c)

        @block.tensor
        def _(pe):
            def turn4(dst, src):
                for j in range(4):
                    ins = nc.tensor.transpose(dst[:, j * P:(j + 1) * P], src(j), ident[:, :])
                return ins

            def project(u, k, part, c):
                if not (isinstance(u, int) and u < 2):
                    pe.wait_ge(aux_free, u - 1)
                w = WQ if part else WK
                nc.tensor.matmul(aux(k), wp[:, w:w + P], xnT[:, c * CH:(c + 1) * CH],
                                 start=True, stop=True).then_inc(aux_full, 1)

            def project_out(dst, c):
                for j in range(4):
                    t = 4 * c + j
                    ins = nc.tensor.matmul(dst[:, j * P:(j + 1) * P], heads_out[:, t * P:(t + 1) * P], wo[:, :],
                                           start=True, stop=True)
                return ins

            def value(u, k, g):
                pe.wait_ge(aux_free, u - 1)
                for j in range(4):
                    t = 4 * g + j
                    ins = nc.tensor.matmul(aux(k)[:, j * P:(j + 1) * P], xnT[:, t * P:(t + 1) * P], wp[:, WV:WV + P],
                                           start=True, stop=True)
                ins.then_inc(aux_full, 1)

            def chunk_scores(u, k, e, b, i):
                t, c = b * (T // 2) + i // plan.chunks, i % plan.chunks
                pe.wait_ge(aux_free, u - 1)
                nc.tensor.matmul(aux(k), queries_hi[e][:, t * P:(t + 1) * P], keys_full[e][:, c * CH:(c + 1) * CH],
                                 start=True, stop=True).then_inc(aux_full, 1)

            def turn_max(u, k, b, count):
                pe.wait_ge(aux_free, u - 1)
                pe.wait_ge(row_max_ready, count)
                nc.tensor.transpose(aux(k)[0:T // 2, 0:P], row_max[:, b, :], ident[:, :]).then_inc(aux_full, 1)

            def scores_chunk(g, n, c):
                hs = n % S
                e, b, jt = hs // HS, hs % HS // T, hs % T
                keys = slice(jt * P, (jt + 1) * P)
                cols = slice(b * QB + c * CH, b * QB + (c + 1) * CH)
                out = ps[:, 2 * (n % 2) + c, :]
                nc.tensor.matmul(out, keys_full[e][:, keys], queries_hi[e][:, cols], start=True, stop=False)
                return nc.tensor.matmul(out, keys_hi[e][:, keys], queries_lo[e][:, cols], start=False, stop=True)

            def pv_chunk(n, c):
                e, jt = n // HS, n % T
                first, final = jt == 0, jt == T - 1
                out = ps[:, PV + c, :]
                hi = probs_hi[:, n % 4, c * CH:(c + 1) * CH]
                nc.tensor.matmul(out, values_hi[e][:, jt, :], hi, start=first, stop=False)
                nc.tensor.matmul(out[0:DH + 1, :], values_lo[e][:, jt, :], hi, start=False, stop=False)
                return nc.tensor.matmul(out, values_hi[e][:, jt, :], probs_lo[:, n % 4, c * CH:(c + 1) * CH],
                                        start=False, stop=final)

            pe.wait_ge(ident_in_sem, 16)
            for c in range(4):
                pe.wait_ge(normed[XLN], c + 1)
                turn4(ps[:, c, :], lambda j: xn[:, 4 * c + j, :]).then_inc(xT_full, 1)
                if c == 1:
                    pe.wait_ge(wp_in, 16)
                if c > 0:
                    pe.wait_ge(xnT_ready, c)
                    project(c - 1, c - 1, 1, c - 1)
            pe.wait_ge(xnT_ready, 4)
            project(3, 3, 1, 3)
            for c in range(4):
                project(4 + c, 4 + c, 0, c)
            for g in range(4):
                value(8 + g, 8 + g, g)
            pe.wait_ge(first_in, 96)
            pe.wait_ge(head_in[0], 64)
            for i in range(HALF // 2):
                if i < 2:
                    pe.wait_ge(xnT_ready, 4)
                elif i > 2:
                    pe.wait_ge(first_free, i - 2)
                t, half = divmod(i, 2)
                for c in range(2):
                    cols = slice((2 * half + c) * CH, (2 * half + c + 1) * CH)
                    ins = nc.tensor.matmul(first_banks(i)[:, c, :], queries_hi[0][:, t * P:(t + 1) * P],
                                           keys_full[0][:, cols], start=True, stop=True)
                ins.then_inc(first_full, 1)
            turn_max(12, 12, 0, 1)
            pe.wait_ge(first_free, HALF // 2)
            pe.wait_ge(rest_in[0], 32)
            for i in range(EARLY):
                if i == EARLY // 2:
                    pe.wait_ge(max_in[0], 16)
                    for n in range(2):
                        scores_chunk(n, n, 0)
                        scores_chunk(n, n, 1).then_inc(scores_ready, 1)
                chunk_scores(13 + i, 13 + i, 0, 1, i)

            def unit(kind, args, p, u, k):
                if kind == "max":
                    e, b, i = args
                    if i == 0 and b == 0:
                        pe.wait_ge(head_in[e], p * 64 + (64 if e == 1 else 128))
                    chunk_scores(u, k, e, b, i)
                elif kind == "max_row":
                    e, b = args
                    turn_max(u, k, b, p * 4 + {(0, 1): 2, (1, 0): 3, (1, 1): 4, (0, 0): 5}[e, b])
                elif kind == "project":
                    if args == [0, 0]:
                        pe.wait_ge(wp_in, p * 16 + 32)
                    project(u, k, *args)
                elif kind == "value":
                    value(u, k, *args)
                elif kind == "last_out":
                    pe.wait_ge(aux_free, u - 1)
                    pe.wait_ge(heads_ready, PAIRS * 4 + 1)
                    pe.wait_ge(wo_in, 16 * (PAIRS + 1))
                    project_out(aux(k), args[0]).then_inc(aux_full, 1)
                elif kind == "out":
                    pe.wait_ge(aux_free, u - 1)
                    if args[0] == 0:
                        pe.wait_ge(heads_ready, p * 4 + 2)
                        pe.wait_ge(wo_in, p * 16 + 16)
                    project_out(aux(k), args[0]).then_inc(aux_full, 1)

            def pair(p, units, last):
                base, local = p * U + U0, 0
                for n in range(S):
                    g = p * S + n
                    work = [(u, base + local + i, U0 + local + i) for i, u in enumerate(units[n])]
                    local += len(work)

                    def aux_unit():
                        if work:
                            (kind, *args), u, k = work.pop(0)
                            unit(kind, args, p, u, k)

                    if not (last and n + 2 >= S):
                        m = (n + 2) % S
                        if m % T == 0:
                            e, b = m // HS, m % HS // T
                            if b == 0:
                                pe.wait_ge(rest_in[e], (p + (n + 2) // S) * 32 + 32)
                            pe.wait_ge(max_in[e], (p + (n + 2) // S) * 32 + 16 * (b + 1))
                        pe.wait_ge(probs_ready, g + 1)
                        scores_chunk(g + 2, m, 0)
                        scores_chunk(g + 2, m, 1).then_inc(scores_ready, 1)
                    aux_unit()
                    if n % HS == 0:
                        pe.wait_ge(v_lo, p * 2 + 1 + n // HS)
                    if n % T == 0:
                        pe.wait_ge(half_out, p * 4 + n // T + 1)
                    pe.wait_ge(lo_ready, g + 1)
                    half = pv_chunk(n, 0)
                    if n % T == T - 1:
                        half.then_inc(half_done, 1)
                    aux_unit()
                    if n % T == 0:
                        pe.wait_ge(numer_ready, p * 4 + n // T + 1)
                    pv_chunk(n, 1).then_inc(pv_done, 1)
                    while work:
                        aux_unit()

            with pe.Fori(0, PAIRS - 1) as p:
                pair(p, units, False)
            pair(PAIRS - 1, units_last, True)

            def weight(i):
                return ffn[:, i * P:(i + 1) * P]

            def gate(c, k):
                nc.tensor.matmul(bank(c, GATE[k]), weight(k), xnT[:, c * CH:(c + 1) * CH],
                                 start=True, stop=True).then_inc(gate_full, 1)

            for stage, c in plan.tail():
                cols = slice(c * CH, (c + 1) * CH)
                if stage == "const":
                    pe.wait_ge(vec_in, 16)
                    pe.wait_ge(ffn_in, 16)
                    pe.wait_ge(aux_free, U_LAST)
                    for k in range(3):
                        ins = nc.tensor.matmul(ps[:, CONST, k:k + 1], weight(4 + k), vec[:, 3:4], start=True, stop=True)
                    ins.then_inc(gate_const, 1)
                elif stage == "out":
                    pe.wait_ge(heads_ready, PAIRS * 4 + c)
                    project_out(bank(c, OUT), c).then_inc(out_full, 1)
                elif stage == "zT":
                    pe.wait_ge(normed[ZLN], c + 1)
                    if c == 0:
                        pe.wait_ge(probs_ready, PAIRS * S)
                    if c == 3:
                        pe.wait_ge(gate_const_ready, 1)
                    turn4(bank(c, ZT), lambda j: xn[:, 4 * c + j, :]).then_inc(z_turned, 1)
                elif stage in ("gate_f", "gate_i", "gate_g"):
                    if stage == "gate_i":
                        pe.wait_ge(zT_ready, c + 1)
                    if stage == "gate_f":
                        pe.wait_ge(gates_ready, len(gates_before("gate_i", c)) + 1)
                    gate(c, ("gate_f", "gate_i", "gate_g").index(stage))
                elif stage == "h_z":
                    pe.wait_ge(gates_ready, len(gates_before("gate_g", c)) + 1)
                    nc.tensor.matmul(bank(c, HID), ones_row, bo_row, start=True, stop=False)
                    for j in range(4):
                        t = 4 * c + j
                        nc.tensor.matmul(bank(c, HID)[:, j * P:(j + 1) * P], xnT[:, t * P:(t + 1) * P], weight(3),
                                         start=False, stop=False)
                elif stage == "h":
                    pe.wait_ge(c_ready, c + 1)
                    for j in range(4):
                        t = 4 * c + j
                        ins = nc.tensor.matmul(bank(c, HID)[:, j * P:(j + 1) * P], new_c[:, t * P:(t + 1) * P],
                                               weight(7), start=False, stop=j == 3)
                    ins.then_inc(h_full, 1)


def kernel(**inputs):
    import numpy as np
    import concourse.bacc as bacc
    from concourse.bass_utils import run_bass_kernel_spmd

    a = {k.removeprefix("L0_"): np.asarray(v) for k, v in inputs.items()}
    x = a["attn_x"]
    inner = a["attn_out_w"].shape[1]
    pairs = inner // P
    wT = a["attn_W_w"].T.reshape(P, 3, pairs, P)
    b = a["attn_W_b"].reshape(3, pairs, P)
    w_pair = np.stack([np.concatenate([wT[:, 0, p], wT[:, 1, p], wT[:, 2, p],
                                       np.broadcast_to(b[2, p], (P, P)),
                                       b[0, p][:, None], b[1, p][:, None]], axis=1) for p in range(pairs)])
    arrays = {
        "x": np.ascontiguousarray(x[0]),
        "w_pair": np.ascontiguousarray(w_pair),
        "w_out": np.ascontiguousarray(a["attn_out_w"].T),
        "w_ffn": np.ascontiguousarray(np.concatenate(
            [a["ffn_" + k].T for k in ("wf", "wi", "wc", "wo", "uf", "ui", "uc", "uo")]
            + [np.broadcast_to(a["ffn_bo"], (P, P))] * (CH // P) + [np.ones((P, P), np.float32)], axis=1)),
        "vecs": np.ascontiguousarray(np.concatenate(
            [a[k][:, None] for k in ("ffn_bf", "ffn_bi", "ffn_bc", "ffn_in_c")]
            + [np.broadcast_to(a["attn_out_b"], (P, P))], axis=1)),
        "ident": np.eye(P, dtype=np.float32),
    }
    nc = bacc.Bacc("TRN2", target_bir_lowering=False, num_devices=1)
    arrays = {f"in_{k}_dram": v for k, v in arrays.items()}
    args = [nc.dram_tensor(k, v.shape, F32, kind="ExternalInput").ap() for k, v in arrays.items()]
    y = nc.dram_tensor("out_dram", x.shape[1:], F32, kind="ExternalOutput").ap()
    bass_attention_then_gated_step(nc, *args, y)
    r = run_bass_kernel_spmd(nc, [arrays], core_ids=[0])
    return r.results[0]["out_dram"].reshape(x.shape)
```
